# Optimizing a Trainium2 kernel written in Bass

```python
import numpy as np
import jax
import jax.numpy as jnp

def _softmax(x, axis=-1):
    return jax.nn.softmax(x, axis=axis)

def _gelu(x):
    return jax.nn.gelu(x, approximate=True)

def _silu(x):
    return jax.nn.silu(x)

def _sigmoid(x):
    return jax.nn.sigmoid(x)

def _layernorm(x, axis=-1, eps=1e-05):
    m = jnp.mean(x, axis=axis, keepdims=True)
    v = jnp.var(x, axis=axis, keepdims=True)
    return (x - m) / jnp.sqrt(v + eps)

def _scatter_add(tgt, idx, src, axis=0):
    return tgt.at[idx].add(src)

def _segment_sum(src, seg, n):
    return jax.ops.segment_sum(src, seg, n)
kernel_name = 'mk_xattn_seq_d2_seqx_r4_f7166e'

def setup_inputs(seed: int=0):
    np.random.seed(seed)
    _w = jnp.asarray

    def _rec_inputs():
        import jax
        import jax.numpy as jnp
        _rk = jax.random.key(seed)
        x = -0.0001108 + 0.9999 * jax.random.normal(jax.random.fold_in(_rk, 1), (64, 256, 320), jnp.float32)
        _lenS = 256 - jax.random.randint(jax.random.fold_in(_rk, 7), (64,), 0, max(1, 256 // 4) + 1, jnp.int32)
        _lenS2 = 77 - jax.random.randint(jax.random.fold_in(_rk, 8), (64,), 0, max(1, 77 // 4) + 1, jnp.int32)
        _ctx_2048P = jax.random.normal(jax.random.fold_in(_rk, 11), (64, 16, 512), jnp.float32)
        _ctx_2048c = jax.random.dirichlet(jax.random.fold_in(_rk, 511), 0.3 * jnp.ones((16,), jnp.float32), (64, 77))
        _ctx_2048t = jnp.einsum('bsk,bkd->bsd', _ctx_2048c, _ctx_2048P)
        _ctx_2048t = _ctx_2048t * jax.lax.rsqrt(jnp.mean(jnp.square(_ctx_2048t)) + 1e-12) * 0.953939
        ctx_2048 = -0.000395056 + 1.00006 * (_ctx_2048t + 0.3 * jax.random.normal(jax.random.fold_in(_rk, 611), (64, 77, 512), jnp.float32))
        fside_S_0 = jax.random.uniform(jax.random.fold_in(_rk, 12), (256,), jnp.float32, 0.0, 0.999706)
        return (x, ctx_2048, fside_S_0)
    x, ctx_2048, fside_S_0 = _rec_inputs()

    def _L0_xattn_setup():
        import jax, jax.numpy as jnp
        import numpy as np
        NUM_HEADS = 20
        TEXT_LEN = 77
        IP_SCALE = 1.0

        def _attend(q, k, v, sm_scale):
            scores = jnp.einsum('bhsd,bhld->bhsl', q, k) * sm_scale
            probs = jax.nn.softmax(scores, axis=-1)
            return jnp.einsum('bhsl,bhld->bhsd', probs, v)

        def _split_heads(x, h):
            b, s, c = x.shape
            return x.reshape(b, s, h, c // h).transpose(0, 2, 1, 3)

        def _merge_heads(x):
            b, h, s, d = x.shape
            return x.transpose(0, 2, 1, 3).reshape(b, s, h * d)
        key = jax.random.key(seed)
        ks = jax.random.split(key, 8)
        B, S, C, CC, L = (8, 1024, 320, 512, TEXT_LEN + 4)
        sd_q = 1.0 / np.sqrt(C)
        sd_kv = 1.0 / np.sqrt(CC)
        return {'hidden_states': jax.random.normal(ks[0], (B, S, C), jnp.float32), 'encoder_hidden_states': jax.random.normal(ks[1], (B, L, CC), jnp.float32), 'Wq': jax.random.normal(ks[2], (C, C), jnp.float32) * sd_q, 'Wk': jax.random.normal(ks[3], (C, CC), jnp.float32) * sd_kv, 'Wv': jax.random.normal(ks[4], (C, CC), jnp.float32) * sd_kv, 'Wk_ip': jax.random.normal(ks[5], (C, CC), jnp.float32) * sd_kv, 'Wv_ip': jax.random.normal(ks[6], (C, CC), jnp.float32) * sd_kv, 'Wo': jax.random.normal(ks[7], (C, C), jnp.float32) * sd_q, 'bo': jnp.zeros((C,), jnp.float32)}
    _L0_xattn_all = _L0_xattn_setup()
    _L0_xattn_in = {k: v for k, v in _L0_xattn_all.items() if k in ('Wq', 'Wk', 'Wv', 'Wk_ip', 'Wv_ip', 'Wo', 'bo')}
    del _L0_xattn_all

    def _L1_xattn_setup():
        import jax, jax.numpy as jnp
        import numpy as np
        HEADS = 20
        NUM_TOKENS = 4
        IP_SCALE = 1.0
        SEM_SCALE = 0.5
        RESCALE = 1.0
        EPS = 1e-12

        def _l2norm(x, axis=-1):
            n = jnp.sqrt(jnp.sum(x * x, axis=axis, keepdims=True))
            return x / jnp.maximum(n, EPS)
        key = jax.random.key(seed)
        ks = jax.random.split(key, 10)
        B, S, C = (2, 256, 320)
        T, E = (81, 512)
        inp = {'hidden_states': jax.random.normal(ks[0], (B, S, C), jnp.float32), 'encoder_hidden_states': jax.random.normal(ks[1], (B, T, E), jnp.float32), 'spatial_mask': jax.random.uniform(ks[2], (S,), jnp.float32), 'W_q': jax.random.normal(ks[3], (C, C), jnp.float32) * C ** (-0.5), 'W_k': jax.random.normal(ks[4], (E, C), jnp.float32) * E ** (-0.5), 'W_v': jax.random.normal(ks[5], (E, C), jnp.float32) * E ** (-0.5), 'W_k_ip': jax.random.normal(ks[6], (E, C), jnp.float32) * E ** (-0.5), 'W_v_ip': jax.random.normal(ks[7], (E, C), jnp.float32) * E ** (-0.5), 'W_out': jax.random.normal(ks[8], (C, C), jnp.float32) * C ** (-0.5), 'b_out': jnp.zeros((C,), jnp.float32)}
        return inp
    _L1_xattn_all = _L1_xattn_setup()
    _L1_xattn_in = {k: v for k, v in _L1_xattn_all.items() if k in ('W_q', 'W_k', 'W_v', 'W_k_ip', 'W_v_ip', 'W_out', 'b_out')}
    del _L1_xattn_all
    return {'x': x, 'ctx_2048': ctx_2048, 'fside_S_0': fside_S_0, 'L0_xattn_Wq': _L0_xattn_in['Wq'], 'L0_xattn_Wk': _L0_xattn_in['Wk'], 'L0_xattn_Wv': _L0_xattn_in['Wv'], 'L0_xattn_Wk_ip': _L0_xattn_in['Wk_ip'], 'L0_xattn_Wv_ip': _L0_xattn_in['Wv_ip'], 'L0_xattn_Wo': _L0_xattn_in['Wo'], 'L0_xattn_bo': _L0_xattn_in['bo'], 'L1_xattn_W_q': _L1_xattn_in['W_q'], 'L1_xattn_W_k': _L1_xattn_in['W_k'], 'L1_xattn_W_v': _L1_xattn_in['W_v'], 'L1_xattn_W_k_ip': _L1_xattn_in['W_k_ip'], 'L1_xattn_W_v_ip': _L1_xattn_in['W_v_ip'], 'L1_xattn_W_out': _L1_xattn_in['W_out'], 'L1_xattn_b_out': _L1_xattn_in['b_out']}

def reference(x, ctx_2048, fside_S_0, L0_xattn_Wq, L0_xattn_Wk, L0_xattn_Wv, L0_xattn_Wk_ip, L0_xattn_Wv_ip, L0_xattn_Wo, L0_xattn_bo, L1_xattn_W_q, L1_xattn_W_k, L1_xattn_W_v, L1_xattn_W_k_ip, L1_xattn_W_v_ip, L1_xattn_W_out, L1_xattn_b_out):
    import jax
    import jax.numpy as jnp

    def _L0_xattn_ref(hidden_states, encoder_hidden_states, Wq, Wk, Wv, Wk_ip, Wv_ip, Wo, bo):
        import jax, jax.numpy as jnp
        import numpy as np
        NUM_HEADS = 20
        TEXT_LEN = 77
        IP_SCALE = 1.0

        def _attend(q, k, v, sm_scale):
            scores = jnp.einsum('bhsd,bhld->bhsl', q, k) * sm_scale
            probs = jax.nn.softmax(scores, axis=-1)
            return jnp.einsum('bhsl,bhld->bhsd', probs, v)

        def _split_heads(x, h):
            b, s, c = x.shape
            return x.reshape(b, s, h, c // h).transpose(0, 2, 1, 3)

        def _merge_heads(x):
            b, h, s, d = x.shape
            return x.transpose(0, 2, 1, 3).reshape(b, s, h * d)
        residual = hidden_states
        B, S, C = hidden_states.shape
        H = NUM_HEADS
        D = C // H
        sm_scale = 1.0 / jnp.sqrt(jnp.asarray(D, hidden_states.dtype))
        text = encoder_hidden_states[:, :TEXT_LEN, :]
        ip = encoder_hidden_states[:, TEXT_LEN:, :]
        q = _split_heads(hidden_states @ Wq.T, H)
        k = _split_heads(text @ Wk.T, H)
        v = _split_heads(text @ Wv.T, H)
        out_text = _merge_heads(_attend(q, k, v, sm_scale))
        k_ip = _split_heads(ip @ Wk_ip.T, H)
        v_ip = _split_heads(ip @ Wv_ip.T, H)
        out_ip = _merge_heads(_attend(q, k_ip, v_ip, sm_scale))
        out = out_text + IP_SCALE * out_ip
        out = out @ Wo.T + bo
        return out + residual

    def _L1_xattn_ref(hidden_states, encoder_hidden_states, spatial_mask, W_q, W_k, W_v, W_k_ip, W_v_ip, W_out, b_out):
        import jax, jax.numpy as jnp
        import numpy as np
        HEADS = 20
        NUM_TOKENS = 4
        IP_SCALE = 1.0
        SEM_SCALE = 0.5
        RESCALE = 1.0
        EPS = 1e-12

        def _l2norm(x, axis=-1):
            n = jnp.sqrt(jnp.sum(x * x, axis=axis, keepdims=True))
            return x / jnp.maximum(n, EPS)
        B, S, C = hidden_states.shape
        H = HEADS
        Dh = C // H
        attn_scale = Dh ** (-0.5)
        residual = hidden_states
        text_ehs = encoder_hidden_states[:, :-NUM_TOKENS]
        ip_ehs = encoder_hidden_states[:, -NUM_TOKENS:]

        def heads(x):
            return x.reshape(B, -1, H, Dh).transpose(0, 2, 1, 3)
        q = heads(hidden_states @ W_q)
        k_t = heads(text_ehs @ W_k)
        v_t = heads(text_ehs @ W_v)
        scores_t = jnp.einsum('bhsd,bhtd->bhst', q, k_t) * attn_scale
        probs_t = jax.nn.softmax(scores_t, axis=-1)
        text_out = jnp.einsum('bhst,bhtd->bhsd', probs_t, v_t)
        text_out = text_out.transpose(0, 2, 1, 3).reshape(B, S, C)
        k_ip = heads(ip_ehs @ W_k_ip)
        v_ip = heads(ip_ehs @ W_v_ip)
        attn_scores = jnp.einsum('bhsd,bhnd->bhsn', q, k_ip) * attn_scale
        qsem = jnp.einsum('bhst,bte->bhse', probs_t, text_ehs)
        qsem = _l2norm(qsem)
        ip_n = _l2norm(ip_ehs)
        sem = jnp.einsum('bhse,bne->bhsn', qsem, ip_n)
        sem = jax.lax.stop_gradient(sem)
        fused = attn_scores + SEM_SCALE * sem
        probs_ip = jax.nn.softmax(fused, axis=-1)
        probs_ip = probs_ip * spatial_mask[None, None, :, None]
        ip_out = jnp.einsum('bhsn,bhnd->bhsd', probs_ip, v_ip)
        ip_out = ip_out.transpose(0, 2, 1, 3).reshape(B, S, C)
        out = text_out + IP_SCALE * ip_out
        out = out @ W_out + b_out
        out = out + residual
        return out / RESCALE
    x = _L0_xattn_ref(x, ctx_2048, L0_xattn_Wq, L0_xattn_Wk, L0_xattn_Wv, L0_xattn_Wk_ip, L0_xattn_Wv_ip, L0_xattn_Wo, L0_xattn_bo)
    x = _L1_xattn_ref(x, ctx_2048, fside_S_0, L1_xattn_W_q, L1_xattn_W_k, L1_xattn_W_v, L1_xattn_W_k_ip, L1_xattn_W_v_ip, L1_xattn_W_out, L1_xattn_b_out)
    return x

_drawn_inputs = setup_inputs


def setup_inputs(seed=0):
    import zlib

    import numpy as np

    out = dict(_drawn_inputs(seed))
    spreads = {'L0_xattn_bo': (0.0, 0.1), 'L1_xattn_b_out': (0.0, 0.1)}
    factors = {}
    for name, (base, spread) in spreads.items():
        noise = np.random.default_rng([zlib.crc32(name.encode()), seed]).standard_normal(out[name].shape)
        drawn = base * np.exp(spread * noise) if base else spread * noise
        out[name] = jnp.asarray(drawn.astype(out[name].dtype))
    for name, factor in factors.items():
        out[name] = (out[name] * factor).astype(out[name].dtype)
    return out
```

```python
from contextlib import ExitStack

import numpy as np

import concourse.bass as bass
from concourse import mybir

F32 = mybir.dt.float32
F16 = mybir.dt.float16
I32 = mybir.dt.int32
ACT = mybir.ActivationFunctionType
ALU = mybir.AluOpType
AX_X = mybir.AxisListType.X

P = 128
B, S, C = 64, 256, 320
E = 512
H = 20
D = C // H
T = 77
IP = 4
TXT = (T, T - IP)
GH = 4
G = H // GH
HALF = GH * D
SC = S // P
EC = E // P
CC = [(0, 128), (128, 128), (256, 64)]
PAIR = 2
NP = H // PAIR
VW = (D + 1, D + 1 + T)
QH = 5
NQ = H // QH
SM = float(D) ** -0.5
EPS = 1e-12
GS = 1.0 / 64
RING = 4
MAGIC = 0x5F3759DF
NEWTON = 4


class Batch:

    def __init__(self, i, off=0):
        self.i, self.off = i, off
        self.fixed = isinstance(i, int)

    def at(self, each, k):
        if each == 1:
            return self.i + (self.off + k)
        return self.i * each + (self.off * each + k)

    def index(self):
        return self.i + self.off

    def reached(self, eng, sem, each, k):
        if self.fixed and self.at(each, k) <= 0:
            return
        eng.wait_ge(sem, self.at(each, k))


class Bank:

    def __init__(self, names):
        self.of = {n: (k % RING, k // RING) for k, n in enumerate(names)}
        self.each = [sum(v[0] == r for v in self.of.values()) for r in range(RING)]


def uses(layer):
    names = ["k", "v"] + (["g"] if layer else []) + ["kt"] + [f"q{c}" for c in range(3)]
    names += [f"s{n}" for n in range(SC * G)] + ["m"]
    names += [f"t{p}" for p in range(NP)]
    names += [f"a{n}" for n in range(SC * NQ if layer else SC)]
    names += (["pt"] + [f"ip{s}" for s in range(SC)]) if layer else []
    names += [f"x{c}" for c in range(3)] + [f"o{c}" for c in range(3)]
    return names


def merge(a, b):
    out, j = [], 0
    for n, s in enumerate(a):
        out.append(s)
        upto = (n + 1) * len(b) // len(a)
        out += b[j:upto]
        j = upto
    return out + b[j:]


def head_steps(layer, off):
    st = [("k", 0), ("v", 0)] + ([("g", 0)] if layer else []) + [("q", 0), ("kt", 0), ("q", 1), ("q", 2)]
    st += [("s", n) for n in range(SC * G)] + [("m", 0)]
    return [(layer, off, name, n) for name, n in st]


def score_steps(layer, off):
    return [(layer, off, "t", p) for p in range(NP)]


def tail_steps(layer, off):
    st = [("a", n) for n in range(SC * NQ if layer else SC)]
    st += [("sem", 0), ("pt", 0)] + [("ip", s) for s in range(SC)] if layer else [("norm", 0)]
    st += [("x", c) for c in range(3)] + [("o", c) for c in range(3)]
    return [(layer, off, name, n) for name, n in st]


def body_steps(l0, l1, more):
    a = merge(score_steps(0, 0) if l0 else [], head_steps(1, -1) if l1 else [])
    b = merge(score_steps(1, -1) if l1 else [], tail_steps(0, 0) if l0 else [])
    c = merge(tail_steps(1, -1) if l1 else [], head_steps(0, 1) if more else [])
    return a + b + c


def attention_stack_kernel(nc, x, ctx, ctxip, mask, wq, wk, wv, wo, bias, wk_ip, wv_ip, ident_d, headmask_d,
                           ipmask_d, ind_d, out):
    vip_dram = nc.dram_tensor("vip_dram", (B * IP, C), F32, kind="Internal").ap()
    with ExitStack() as stack:
        def sb(name, shape, dt=F32):
            return stack.enter_context(nc.sbuf_tensor(name, shape, dt))

        def sem(name):
            return stack.enter_context(nc.semaphore(name))

        both = (0, 1)
        ring = [stack.enter_context(nc.psum_tensor(f"ring{l}", [P, RING, 512], F32)) for l in both]
        banks = [Bank(uses(l)) for l in both]

        ident = sb("ident", [P, P])
        ident16 = sb("ident16", [P, P], F16)
        ones = sb("ones", [P, P])
        headmask = sb("headmask", [P, GH], F16)
        ipmask = sb("ipmask", [H * IP, H])
        ind = sb("ind", [P, H, T], F16)
        wq_sb = [sb(f"wq{l}", [P, 3, C]) for l in both]
        wk_sb = [sb(f"wk{l}", [P, EC, C]) for l in both]
        wv_sb = [sb(f"wv{l}", [P, EC, C]) for l in both]
        wo_sb = [sb(f"wo{l}", [P, 3, C]) for l in both]
        bias_sb = [sb(f"bias{l}", [P, 3]) for l in both]
        est = sb("est", [P, SC, H, TXT[1]])
        wki_sb = est[:].rearrange("p s h t -> p (s h t)")[:, 0:EC * 2 * C].rearrange("p (k n) -> p k n", k=EC)
        wvi_sb = sb("wvi", [P, EC, C])
        mask_sb = sb("mask_sb", [P, SC])
        ctxip_sb = sb("ctxip_sb", [P, EC, B * IP])
        ipsq = sb("ipsq", [P, EC, B * IP])
        kih = sb("kih", [P, B, G, IP], F16)
        kil = sb("kil", [P, B, G, IP], F16)
        vip = sb("vip", [P, 2, C])
        ipss = sb("ipss", [P, B * IP])
        ipy = sb("ipy", [P, B * IP])
        ipt = sb("ipt", [P, B * IP])
        rnorm4 = sb("rnorm4", [P, B, IP])
        xin = [sb("x0", [P, 3, S]), sb("x1", [P, 3, S])]
        res = [sb(f"res{l}", [P, 3, S]) for l in both]
        cx = [sb(f"cx{l}", [P, EC, T]) for l in both]
        kn = [sb(f"kn{l}", [P, G, 2, HALF]) for l in both]
        kh = [sb(f"kh{l}", [P, G, T], F16) for l in both]
        kl = [sb(f"kl{l}", [P, G, T], F16) for l in both]
        kbh = [sb(f"kbh{l}", [P, H, T], F16) for l in both]
        kbl = [sb(f"kbl{l}", [P, H, T], F16) for l in both]
        vh = [sb(f"vh{l}", [P, H, VW[l]], F16) for l in both]
        vl = [sb(f"vl{l}", [P, H, VW[l]], F16) for l in both]
        gh = sb("gh", [P, T], F16)
        gl = sb("gl", [P, T], F16)
        qs = [sb(f"qs{l}", [P, G, S], F16) for l in both]
        nm = [sb(f"nm{l}", [P, SC, H]) for l in both]
        mhl = [sb(f"mhl{l}", [P, SC, P], F16) for l in both]
        mt = [sb(f"mt{l}", [P, S], F16) for l in both]
        ef = [sb(f"ef{l}", [P, 2, PAIR * S]) for l in both]
        eh = [sb(f"eh{l}", [P, H, S], F16) for l in both]
        el = [sb(f"el{l}", [P, H, S], F16) for l in both]
        rd = [sb(f"rd{l}", [P, SC, H]) for l in both]
        at = [sb(f"at{l}", [P, SC, 3 * P]) for l in both]
        att = [sb(f"att{l}", [P, 3, S]) for l in both]
        sip = sb("sip", [P, SC, H, IP])
        ust = sb("ust", [P, SC, H, D + 1])
        ast = sb("ast", [P, SC, H, IP])
        pe_ = sb("pe_", [P, 2, QH, TXT[1]])
        n2 = sb("n2", [P, SC, H])
        ny = sb("ny", [P, SC, H])
        nt = sb("nt", [P, SC, H])
        lim = sb("lim", [P, SC, H])
        fu = sb("fu", [P, SC, H, IP])
        fm = sb("fm", [P, SC, H])
        pip = sb("pip", [P, SC, H, IP])
        pt = sb("pt", [H * IP, S])
        viprow = sb("viprow", [H * IP, C])
        vbip = sb("vbip", [H * IP, C])
        outt = sb("outt", [P, 3, S])

        filled = [[sem(f"filled{l}_{r}") for r in range(RING)] for l in both]
        freed = [[sem(f"freed{l}_{r}") for r in range(RING)] for l in both]
        s_w = sem("weights_loaded")
        s_preset = sem("presets_written")
        s_setup = sem("setup_filled")
        s_setup_read = sem("setup_read")
        s_vip_read = sem("setup_values_read")
        s_ipsq = sem("ip_squares")
        s_dve_setup = sem("dve_setup")
        s_kih = sem("setup_keys_high")
        s_vip = sem("vip_stored")
        s_x = sem("x_loaded")
        s_c = [sem(f"ctx{l}_loaded") for l in both]
        s_viprow = sem("vip_rows_loaded")
        s_store = sem("out_stored")

        def pair(name):
            return [sem(f"{name}{l}") for l in both]
        s_res = pair("residual_")
        s_kh, s_kb = pair("k_high"), pair("k_blocks")
        s_vh, s_gh, s_gr = pair("v_high"), sem("gram_high"), sem("gram_spread")
        s_qh = pair("q_high")
        s_mx = sem("maxima")
        s_mh, s_ml = pair("max_high"), pair("max_low")
        s_eh, s_el = pair("exp_high"), pair("exp_low")
        s_rd = pair("den_inverse")
        s_sip, s_ast, s_n2 = sem("ip_scores"), sem("ip_products"), sem("square_norms")
        s_semd, s_fe, s_vb = sem("ip_softmax_steps"), sem("ip_exp"), sem("vip_blocks")
        s_at0 = sem("text_attended")
        KB_EACH = (2, 4)
        AV = (SC, SC * NQ)
        SEMD = 15 + 3 * NEWTON

        def bank(l, use):
            return ring[l][:, banks[l].of[use][0], :]

        def wait_fill(eng, l, b, use, before=False):
            r, k = banks[l].of[use]
            b.reached(eng, filled[l][r], banks[l].each[r], k + 1 - (banks[l].each[r] if before else 0))

        def wait_free(eng, l, b, use):
            r, k = banks[l].of[use]
            b.reached(eng, freed[l][r], banks[l].each[r], k)

        def fill_sem(l, use):
            return filled[l][banks[l].of[use][0]]

        def wait_read(eng, l, b, use, before=False):
            r, k = banks[l].of[use]
            b.reached(eng, freed[l][r], banks[l].each[r], k + 1 - (banks[l].each[r] if before else 0))

        def free_sem(l, use):
            return freed[l][banks[l].of[use][0]]

        def program(eng, steps):
            def turn(i, l0, l1, more):
                for layer, off, name, n in body_steps(l0, l1, more):
                    if name in steps:
                        steps[name](layer, Batch(i, off), n)
            for layer, off, name, n in head_steps(0, 0):
                if name in steps:
                    steps[name](layer, Batch(0, off), n)
            turn(0, True, False, True)
            turn(1, True, True, True)
            with eng.Fori(2, B - 1) as i:
                turn(i, True, True, True)
            turn(B - 1, True, True, False)
            turn(B, False, True, False)

        WEIGHTS = 26
        block = stack.enter_context(nc.Block())

        @block.sync
        def _(sp):
            n = 0
            for t, d in [(ident, ident_d), (headmask, headmask_d), (ipmask, ipmask_d),
                         (mask_sb, mask)]:
                sp.dma_start(t[:], d).then_inc(s_w, 16)
                n += 1
            sp.dma_start(ind[:].rearrange("p h t -> p (h t)"), ind_d).then_inc(s_w, 16)
            sp.dma_start(ctxip_sb[:], ctxip.rearrange("(k p) n -> p k n", p=P)).then_inc(s_w, 16)
            n += 2
            for t, d in [(wki_sb, wk_ip), (wvi_sb[:], wv_ip)] + [(wk_sb[l][:], wk[l]) for l in both] + [
                    (wv_sb[l][:], wv[l]) for l in both]:
                sp.dma_start(t, d.rearrange("(k p) n -> p k n", p=P)).then_inc(s_w, 16)
                n += 1
            for t, d in [(wq_sb[l], wq[l]) for l in both] + [(wo_sb[l], wo[l]) for l in both]:
                sp.dma_start(t[:, 0:2, :], d[0:256, :].rearrange("(k p) n -> p k n", p=P)).then_inc(s_w, 16)
                sp.dma_start(t[0:64, 2, :], d[256:320, :]).then_inc(s_w, 16)
                n += 2
            for l in both:
                for c, (c0, m) in enumerate(CC):
                    sp.dma_start(bias_sb[l][0:m, c:c + 1], bias[l][c0:c0 + m, :]).then_inc(s_w, 16)
                    n += 1
            assert n == WEIGHTS

            def load_x(b):
                wait_fill(sp, 0, b, "q2", before=True)
                b.reached(sp, s_res[0], 3, 0)
                src = x[bass.DynSlice(b.index(), 1), :, :].rearrange("a c s -> (a c) s")
                sp.dma_start(xin[0][:, 0:2, :], src[0:256, :].rearrange("(k p) s -> p k s", p=P)).then_inc(s_x, 16)
                sp.dma_start(xin[0][0:64, 2, :], src[256:320, :]).then_inc(s_x, 16)

            def load_ctx(l, b):
                wait_fill(sp, l, b, "g" if l else "v", before=True)
                src = ctx[bass.DynSlice(b.index(), 1), :, :].rearrange("a e t -> (a e) t")
                sp.dma_start(cx[l][:], src.rearrange("(k p) t -> p k t", p=P)).then_inc(s_c[l], 16)

            def load_vip(b):
                b.reached(sp, s_vb, 1, 0)
                src = vip_dram[bass.DynSlice(b.index() * IP, IP), :]
                for h in range(H):
                    sp.dma_start(viprow[h * IP:(h + 1) * IP, :], src).then_inc(s_viprow, 16)

            def store(b):
                wait_read(sp, 1, b, "o2")
                dst = out[bass.DynSlice(b.index(), 1), :, :].rearrange("a c s -> (a c) s")
                sp.dma_start(dst[0:256, :].rearrange("(k p) s -> p k s", p=P), outt[:, 0:2, :]).then_inc(s_store, 16)
                sp.dma_start(dst[256:320, :], outt[0:64, 2, :]).then_inc(s_store, 16)

            load_ctx(0, Batch(0))
            load_x(Batch(0))
            sp.wait_ge(s_vip_read, 2)
            for k in range(2):
                sp.dma_start(vip_dram[k * P:(k + 1) * P, :], vip[:, k, :]).then_inc(s_vip, 16)
            sp.wait_ge(s_vip, 32)

            def turn(i, l0, l1, more):
                if more:
                    load_ctx(0, Batch(i, 1))
                    load_x(Batch(i, 1))
                if l0:
                    load_ctx(1, Batch(i, 0))
                    load_vip(Batch(i, 0))
                if l1:
                    store(Batch(i, -1))
            turn(0, True, False, True)
            turn(1, True, True, True)
            with sp.Fori(2, B - 1) as i:
                turn(i, True, True, True)
            turn(B - 1, True, True, False)
            turn(B, False, True, False)
            sp.wait_ge(s_store, 32 * B)

        @block.tensor
        def _(pe):
            pe.wait_ge(s_w, 16 * WEIGHTS)
            pe.wait_ge(s_preset, 1)
            for g in range(G):
                if g >= RING:
                    pe.wait_ge(s_setup_read, g - RING + 1)
                for k in range(EC):
                    w = wki_sb[:, k, g * P:(g + 1) * P]
                    mm = pe.matmul(ring[1][:, g % RING, 0:B * IP], w, ctxip_sb[:, k, :],
                                   start=(k == 0), stop=(k == EC - 1))
                mm.then_inc(s_setup, 1)
            for j in range(2):
                pe.wait_ge(s_setup_read, G + j - RING + 1)
                for k in range(EC):
                    mm = pe.matmul(ring[1][:, (G + j) % RING, 0:C], ctxip_sb[:, k, j * P:(j + 1) * P],
                                   wvi_sb[:, k, :], start=(k == 0), stop=(k == EC - 1))
                mm.then_inc(s_setup, 1)
            pe.wait_ge(s_setup_read, G + 2 - RING + 1)
            pe.wait_ge(s_ipsq, 1)
            for k in range(EC):
                mm = pe.matmul(ring[1][:, (G + 2) % RING, 0:B * IP], ones[:], ipsq[:, k, :],
                               start=(k == 0), stop=(k == EC - 1))
            mm.then_inc(s_setup, 1)
            pe.wait_ge(s_setup_read, G + 1)
            pe.wait_ge(s_vip_read, 2)

            def rows(l, b, n):
                wait_free(pe, l, b, "k")
                b.reached(pe, s_c[l], 16, 16)
                for k in range(EC):
                    mm = pe.matmul(bank(l, "k")[0:TXT[l], 0:C], cx[l][:, k, 0:TXT[l]], wk_sb[l][:, k, :],
                                   start=(k == 0), stop=(k == EC - 1))
                mm.then_inc(fill_sem(l, "k"), 1)

            def values(l, b, n):
                wait_free(pe, l, b, "v")
                for k in range(EC):
                    mm = pe.matmul(bank(l, "v")[0:TXT[l], 0:C], cx[l][:, k, 0:TXT[l]], wv_sb[l][:, k, :],
                                   start=(k == 0), stop=(k == EC - 1))
                mm.then_inc(fill_sem(l, "v"), 1)

            def gram(l, b, n):
                wait_free(pe, l, b, "g")
                for k in range(EC):
                    mm = pe.matmul(bank(l, "g")[0:TXT[1], 0:T], cx[l][:, k, 0:TXT[1]], cx[l][:, k, :],
                                   start=(k == 0), stop=(k == EC - 1))
                mm.then_inc(fill_sem(l, "g"), 1)

            def turn_keys(l, b, n):
                wait_free(pe, l, b, "kt")
                wait_read(pe, l, b, "k")
                for g in range(G):
                    k2 = kn[l][0:TXT[l], g, :, :].rearrange("t r c -> t (r c)")
                    mm = pe.transpose(bank(l, "kt")[:, g * T:g * T + TXT[l]], k2, ident[0:TXT[l], 0:TXT[l]])
                mm.then_inc(fill_sem(l, "kt"), 1)

            def query(l, b, c):
                c0, m = CC[c]
                wait_free(pe, l, b, f"q{c}")
                if l == 0:
                    b.reached(pe, s_x, 32, 32)
                else:
                    wait_read(pe, 0, b, "o2")
                for k, (_, kk) in enumerate(CC):
                    mm = pe.matmul(bank(l, f"q{c}")[0:m, 0:S], wq_sb[l][0:kk, k, c0:c0 + m], xin[l][0:kk, k, :],
                                   start=(k == 0), stop=(k == 2))
                mm.then_inc(fill_sem(l, f"q{c}"), 1)

            def scores(l, b, n):
                s, g = divmod(n, G)
                use = f"s{n}"
                wait_free(pe, l, b, use)
                wait_read(pe, l, b, f"q{g // 2}")
                b.reached(pe, s_kb[l], KB_EACH[l], KB_EACH[l])
                o = bank(l, use)[:, 0:GH * T]
                q = qs[l][:, g, s * P:(s + 1) * P]
                pe.matmul(o, q, kbh[l][:, g * GH:(g + 1) * GH, :], start=True, stop=False)
                pe.matmul(o, q, kbl[l][:, g * GH:(g + 1) * GH, :], start=False, stop=True).then_inc(fill_sem(l, use), 1)

            def turn_max(l, b, n):
                wait_free(pe, l, b, "m")
                b.reached(pe, s_ml[l], 1, 1)
                o = bank(l, "m").bitcast(F16)
                for s in range(SC):
                    mm = pe.transpose(o[:, s * P:(s + 1) * P], mhl[l][:, s, :], ident16[:])
                mm.then_inc(fill_sem(l, "m"), 1)

            def turned_scores(l, b, p):
                use = f"t{p}"
                wait_free(pe, l, b, use)
                wait_read(pe, l, b, "m")
                for j in range(PAIR):
                    h = p * PAIR + j
                    o = bank(l, use)[0:TXT[l], j * S:(j + 1) * S]
                    q = qs[l][:, h // GH, :]
                    pe.matmul(o, kbh[l][:, h, 0:TXT[l]], q, start=True, stop=False)
                    pe.matmul(o, kbl[l][:, h, 0:TXT[l]], q, start=False, stop=False)
                    mm = pe.matmul(o, ind[:, h, 0:TXT[l]], mt[l][:], start=False, stop=True)
                mm.then_inc(fill_sem(l, use), 1)

            def attend(l, b, n):
                use = f"a{n}"
                s, q = divmod(n, NQ) if l else (n, 0)
                heads = range(q * QH, (q + 1) * QH) if l else range(H)
                wait_free(pe, l, b, use)
                b.reached(pe, s_eh[l], NP, heads[-1] // PAIR + 1)
                b.reached(pe, s_el[l], NP, heads[-1] // PAIR + 1)
                wait_read(pe, l, b, "v")
                if l:
                    b.reached(pe, s_gr, 2, 2)
                w = VW[l]
                for k, h in enumerate(heads):
                    o = bank(l, use)[:, k * w:(k + 1) * w]
                    e_h, e_l = eh[l][:, h, s * P:(s + 1) * P], el[l][:, h, s * P:(s + 1) * P]
                    pe.matmul(o, e_h, vh[l][:, h, :], start=True, stop=False)
                    pe.matmul(o, e_h, vl[l][:, h, :], start=False, stop=False)
                    mm = pe.matmul(o, e_l, vh[l][:, h, :], start=False, stop=True)
                mm.then_inc(fill_sem(l, use), 1)

            def turn_probs(l, b, n):
                wait_free(pe, l, b, "pt")
                b.reached(pe, s_semd, SEMD, SEMD)
                for s in range(SC):
                    mm = pe.transpose(bank(l, "pt")[0:H * IP, s * P:(s + 1) * P],
                                      pip[:, s, :, :].rearrange("p h n -> p (h n)"), ident[:])
                mm.then_inc(fill_sem(l, "pt"), 1)

            def attend_ip(l, b, s):
                use = f"ip{s}"
                wait_free(pe, l, b, use)
                wait_read(pe, l, b, "pt")
                b.reached(pe, s_vb, 1, 1)
                pe.matmul(bank(l, use)[:, 0:C], pt[:, s * P:(s + 1) * P], vbip[:],
                          start=True, stop=True).then_inc(fill_sem(l, use), 1)

            def turn_attended(l, b, c):
                wait_free(pe, l, b, f"x{c}")
                wait_read(pe, l, b, f"ip{SC - 1}" if l else f"a{SC - 1}")
                for s in range(SC):
                    mm = pe.transpose(bank(l, f"x{c}")[:, s * P:(s + 1) * P], at[l][:, s, c * P:(c + 1) * P], ident[:])
                mm.then_inc(fill_sem(l, f"x{c}"), 1)

            def project(l, b, c):
                c0, m = CC[c]
                wait_free(pe, l, b, f"o{c}")
                wait_read(pe, l, b, "x2")
                for k, (_, kk) in enumerate(CC):
                    mm = pe.matmul(bank(l, f"o{c}")[0:m, 0:S], wo_sb[l][0:kk, k, c0:c0 + m], att[l][0:kk, k, :],
                                   start=(k == 0), stop=(k == 2))
                mm.then_inc(fill_sem(l, f"o{c}"), 1)

            program(pe, {"k": rows, "v": values, "g": gram, "kt": turn_keys, "q": query, "s": scores, "m": turn_max,
                         "t": turned_scores, "a": attend, "pt": turn_probs, "ip": attend_ip, "x": turn_attended,
                         "o": project})

        @block.scalar
        def _(act):
            for g in range(G):
                act.wait_ge(s_setup, g + 1)
                src = ring[1][:, g % RING, 0:B * IP].rearrange("p (b n) -> p b n", n=IP)
                act.activation(kih[:, :, g, :], src, ACT.Copy).then_inc(s_kih, 1)
            for j in range(2):
                act.wait_ge(s_setup, G + j + 1)
                act.activation(vip[:, j, :], ring[1][:, (G + j) % RING, 0:C], ACT.Copy).then_inc(s_vip_read, 1)

            def rows(l, b, n):
                wait_fill(act, l, b, "k")
                wait_fill(act, l, b, "kt", before=True)
                src = bank(l, "k")[0:TXT[l], 0:C].rearrange("t (g c) -> t g c", c=HALF)
                act.activation(kn[l][0:TXT[l], :, :, :], src.unsqueeze(2).to_broadcast([TXT[l], G, 2, HALF]),
                               ACT.Copy).then_inc(free_sem(l, "k"), 1)

            def values(l, b, n):
                wait_fill(act, l, b, "v")
                wait_fill(act, l, b, f"a{AV[l] - 1}", before=True)
                act.activation(vh[l][0:TXT[l], :, 0:D], bank(l, "v")[0:TXT[l], 0:C].rearrange("t (h d) -> t h d", d=D),
                               ACT.Copy).then_inc(s_vh[l], 1)

            def gram(l, b, n):
                wait_fill(act, l, b, "g")
                b.reached(act, s_gr, 2, 0)
                act.activation(gh[0:TXT[1], :], bank(l, "g")[0:TXT[1], 0:T], ACT.Copy, scale=GS).then_inc(s_gh, 1)

            def turn_keys(l, b, n):
                wait_fill(act, l, b, "kt")
                b.reached(act, s_kb[l], KB_EACH[l], 0)
                src = bank(l, "kt")[:, 0:G * T].rearrange("p (g t) -> p g t", t=T)[:, :, 0:TXT[l]]
                act.activation(kh[l][:, :, 0:TXT[l]], src, ACT.Copy).then_inc(s_kh[l], 1)

            def query(l, b, c):
                wait_fill(act, l, b, f"q{c}")
                wait_fill(act, l, b, f"t{NP - 1}", before=True)
                for j in range(CC[c][1] // HALF):
                    act.activation(qs[l][0:HALF, 2 * c + j, :], bank(l, f"q{c}")[j * HALF:(j + 1) * HALF, 0:S],
                                   ACT.Copy, scale=SM).then_inc(s_qh[l], 1)

            def scores(l, b, n):
                if l == 0:
                    return
                s, g = divmod(n, G)
                b.reached(act, s_mx, SC * G, n + 1)
                wait_read(act, 1, b, f"a{AV[1] - 1}", before=True)
                b.reached(act, s_semd, SEMD, 0)
                o = bank(l, f"s{n}")[:, 0:GH * T].rearrange("p (h t) -> p h t", t=T)
                act.activation(sip[:, s, g * GH:(g + 1) * GH, :], o[:, :, TXT[1]:T], ACT.Copy).then_inc(s_sip, 1)
                for j in range(GH):
                    h = g * GH + j
                    ins = act.activation(est[:, s, h, :], o[:, j, 0:TXT[1]], ACT.Exp, bias=nm[1][:, s, h:h + 1])
                ins.then_inc(free_sem(l, f"s{n}"), 1)

            def turn_max(l, b, n):
                wait_fill(act, l, b, "m")
                wait_fill(act, l, b, f"t{NP - 1}", before=True)
                act.activation(mt[l][:], bank(l, "m").bitcast(F16)[:, 0:S], ACT.Copy)\
                   .then_inc(free_sem(l, "m"), 1)

            def turned_scores(l, b, p):
                use = f"t{p}"
                wait_fill(act, l, b, use)
                b.reached(act, s_el[l], NP, p - 1)
                n = TXT[l]
                act.activation(ef[l][0:n, p % 2, :], bank(l, use)[0:n, :], ACT.Exp).then_inc(free_sem(l, use), 1)
                wait_fill(act, l, b, f"a{AV[l] - 1}", before=True)
                wait_read(act, l, b, use)
                act.activation(eh[l][0:n, p * PAIR:(p + 1) * PAIR, :],
                               ef[l][0:n, p % 2, :].rearrange("t (h s) -> t h s", s=S), ACT.Copy).then_inc(s_eh[l], 1)

            def attend(l, b, n):
                if l == 0:
                    return
                s, q = divmod(n, NQ)
                wait_fill(act, l, b, f"a{n}")
                b.reached(act, s_at0, 1, 0)
                o = bank(l, f"a{n}")[:, 0:QH * VW[1]].rearrange("p (h w) -> p h w", w=VW[1])
                act.activation(ust[:, s, q * QH:(q + 1) * QH, :], o[:, :, 0:D + 1], ACT.Copy)
                act.activation(ast[:, s, q * QH:(q + 1) * QH, :], o[:, :, D + 1 + TXT[1]:], ACT.Copy).then_inc(s_ast, 1)

            def fused_exp(l, b, n):
                b.reached(act, s_semd, SEMD, SEMD - 4)
                act.activation(fu[:], fu[:], ACT.Exp).then_inc(s_fe, 1)

            def turn_probs(l, b, n):
                wait_fill(act, l, b, "pt")
                act.activation(pt[:], bank(l, "pt")[0:H * IP, 0:S], ACT.Copy).then_inc(free_sem(l, "pt"), 1)

            def turn_attended(l, b, c):
                m = CC[c][1]
                wait_fill(act, l, b, f"x{c}")
                act.activation(att[l][0:m, c, :], bank(l, f"x{c}")[0:m, 0:S], ACT.Copy)\
                   .then_inc(free_sem(l, f"x{c}"), 1)

            program(act, {"k": rows, "v": values, "g": gram, "kt": turn_keys, "q": query, "s": scores, "m": turn_max,
                          "t": turned_scores, "a": attend, "sem": fused_exp, "pt": turn_probs, "x": turn_attended})

        @block.vector
        def _(dve):
            for l in both:
                for t in (eh[l], el[l], vh[l], vl[l], at[l]):
                    dve.memset(t[:], 0.0).then_inc(s_dve_setup, 1)
                dve.memset(mhl[l][:], 0.0).then_inc(s_dve_setup, 1)
            dve.wait_ge(s_dve_setup, 12)
            for l in both:
                dve.memset(vh[l][0:TXT[l], :, D:D + 1], 1.0).then_inc(s_dve_setup, 1)
            dve.wait_ge(s_dve_setup, 14)
            dve.memset(ones[:], 1.0).then_inc(s_dve_setup, 1)
            dve.wait_ge(s_w, 16 * WEIGHTS)
            dve.tensor_copy(ident16[:], ident[:]).then_inc(s_dve_setup, 1)
            dve.wait_ge(s_dve_setup, 16)
            dve.tensor_tensor(ipsq[:], ctxip_sb[:], ctxip_sb[:], ALU.mult).then_inc(s_ipsq, 1)
            dve.sem_inc(s_preset, 1)
            for g in range(G):
                dve.wait_ge(s_kih, g + 1)
                src = ring[1][:, g % RING, 0:B * IP].rearrange("p (b n) -> p b n", n=IP)
                dve.tensor_tensor(kil[:, :, g, :], src, kih[:, :, g, :], ALU.subtract).then_inc(s_setup_read, 1)

            def inverse_root(eng, sq, y, t):
                yield eng.tensor_scalar(y.bitcast(I32), sq.bitcast(I32), 1, None, ALU.logical_shift_right)
                yield eng.tensor_scalar(y.bitcast(I32), y.bitcast(I32), -1.0, float(MAGIC), ALU.mult, ALU.add)
                for _ in range(NEWTON):
                    yield eng.tensor_tensor(t, y, y, ALU.mult)
                    yield eng.scalar_tensor_tensor(t, t, -0.5, sq, ALU.mult, ALU.mult)
                    yield eng.scalar_tensor_tensor(y, t, 1.5, y, ALU.add, ALU.mult)

            dve.wait_ge(s_setup, G + 3)
            dve.tensor_scalar(ipss[:], ring[1][:, (G + 2) % RING, 0:B * IP], EPS * EPS, None, ALU.max)\
               .then_inc(s_setup_read, 1)
            dve.wait_ge(s_setup_read, G + 1)
            n = 0
            for ins in inverse_root(dve, ipss[:], ipy[:], ipt[:]):
                n += 1
                ins.then_inc(s_ipsq, 1)
                dve.wait_ge(s_ipsq, 1 + n)
            dve.tensor_scalar(rnorm4[:].rearrange("p b n -> p (b n)"), ipy[:], 4.0, None, ALU.mult).then_inc(s_ipsq, 1)
            dve.wait_ge(s_ipsq, 2 + n)

            def values(l, b, n):
                b.reached(dve, s_vh[l], 1, 1)
                src = bank(l, "v")[0:TXT[l], 0:C].rearrange("t (h d) -> t h d", d=D)
                dve.tensor_tensor(vl[l][0:TXT[l], :, 0:D], src, vh[l][0:TXT[l], :, 0:D], ALU.subtract)\
                   .then_inc(free_sem(l, "v"), 1)

            def gram(l, b, n):
                b.reached(dve, s_gh, 1, 1)
                dve.scalar_tensor_tensor(gl[0:TXT[1], :], bank(l, "g")[0:TXT[1], 0:T], GS, gh[0:TXT[1], :],
                                         ALU.mult, ALU.subtract).then_inc(free_sem(l, "g"), 1)
                wait_read(dve, l, b, "g")
                wait_fill(dve, l, b, f"a{AV[l] - 1}", before=True)
                for t, src in ((vh[1], gh), (vl[1], gl)):
                    dve.tensor_copy(t[0:TXT[1], :, D + 1:],
                                    src[0:TXT[1], :].unsqueeze(1).to_broadcast([TXT[1], H, T])).then_inc(s_gr, 1)

            def turn_keys(l, b, n):
                b.reached(dve, s_kh[l], 1, 1)
                src = bank(l, "kt")[:, 0:G * T].rearrange("p (g t) -> p g t", t=T)[:, :, 0:TXT[l]]
                dve.tensor_tensor(kl[l][:, :, 0:TXT[l]], src, kh[l][:, :, 0:TXT[l]], ALU.subtract)\
                   .then_inc(free_sem(l, "kt"), 1)

            def query(l, b, c):
                groups = CC[c][1] // HALF
                for j in range(groups):
                    g = 2 * c + j
                    b.reached(dve, s_qh[l], G, g + 1)
                    ins = dve.scalar_tensor_tensor(qs[l][HALF:P, g, :], bank(l, f"q{c}")[j * HALF:(j + 1) * HALF, 0:S], SM,
                                             qs[l][0:HALF, g, :], ALU.mult, ALU.subtract)
                ins.then_inc(free_sem(l, f"q{c}"), 1)

            def scores(l, b, n):
                s, g = divmod(n, G)
                wait_fill(dve, l, b, f"s{n}")
                if l:
                    wait_fill(dve, l, b, "m", before=True)
                o = bank(l, f"s{n}")[:, 0:GH * T].rearrange("p (h t) -> p h t", t=T)[:, :, 0:TXT[l]]
                dve.tensor_reduce(nm[l][:, s, g * GH:(g + 1) * GH], o, AX_X, ALU.max, negate=True)\
                   .then_inc(s_mx if l else free_sem(l, f"s{n}"), 1)

            def turn_max(l, b, n):
                if l:
                    b.reached(dve, s_mx, SC * G, SC * G)
                else:
                    wait_read(dve, l, b, f"s{SC * G - 1}")
                wait_fill(dve, l, b, "m", before=True)
                dve.tensor_copy(mhl[l][:, :, 0:H], nm[l][:]).then_inc(s_mh[l], 1)
                b.reached(dve, s_mh[l], 1, 1)
                dve.tensor_tensor(mhl[l][:, :, 32:32 + H], nm[l][:], mhl[l][:, :, 0:H], ALU.subtract)\
                   .then_inc(s_ml[l], 1)

            def turned_scores(l, b, p):
                n = TXT[l]
                b.reached(dve, s_eh[l], NP, p + 1)
                dve.tensor_tensor(el[l][0:n, p * PAIR:(p + 1) * PAIR, :],
                                  ef[l][0:n, p % 2, :].rearrange("t (h s) -> t h s", s=S),
                                  eh[l][0:n, p * PAIR:(p + 1) * PAIR, :], ALU.subtract).then_inc(s_el[l], 1)

            def attend(l, b, n):
                if l == 0:
                    wait_fill(dve, l, b, f"a{n}")
                    o = bank(l, f"a{n}")[:, 0:H * VW[0]].rearrange("p (h w) -> p h w", w=VW[0])
                    wait_read(dve, l, b, f"a{n}", before=True)
                    dve.reciprocal(rd[0][:, n, :], o[:, :, D]).then_inc(s_rd[0], 1)
                    b.reached(dve, s_rd[0], SC, n + 1)
                    wait_fill(dve, l, b, "x2", before=True)
                    dve.tensor_tensor(at[0][:, n, 0:C].rearrange("p (h d) -> p h d", d=D), o[:, :, 0:D],
                                      rd[0][:, n, :].unsqueeze(2).to_broadcast([P, H, D]), ALU.mult)\
                       .then_inc(free_sem(l, f"a{n}"), 1)
                    return
                s, q = divmod(n, NQ)
                b.reached(dve, s_ast, SC * NQ, n + 1)
                b.reached(dve, s_n2, SC * NQ, n - 1)
                o = bank(l, f"a{n}")[:, 0:QH * VW[1]].rearrange("p (h w) -> p h w", w=VW[1])
                dve.tensor_tensor(pe_[:, n % 2, :, :], o[:, :, D + 1:D + 1 + TXT[1]], est[:, s, q * QH:(q + 1) * QH, :],
                                  ALU.mult).then_inc(free_sem(l, f"a{n}"), 1)
                wait_read(dve, l, b, f"a{n}")
                dve.tensor_reduce(n2[:, s, q * QH:(q + 1) * QH], pe_[:, n % 2, :, :], AX_X, ALU.add).then_inc(s_n2, 1)

            def semantic(l, b, n):
                count = [0]

                def chain(ins):
                    count[0] += 1
                    ins.then_inc(s_semd, 1)
                    b.reached(dve, s_semd, SEMD, count[0])

                b.reached(dve, s_n2, SC * NQ, SC * NQ)
                den = ust[:, :, :, D]
                wait_fill(dve, l, b, "ip1", before=True)
                dve.reciprocal(rd[1][:], den).then_inc(s_rd[1], 1)
                chain(dve.tensor_scalar(lim[:], den, EPS / 8, None, ALU.mult))
                chain(dve.reciprocal(lim[:], lim[:]))
                chain(dve.tensor_scalar(n2[:], n2[:], 1e-37, None, ALU.max))
                for ins in inverse_root(dve, n2[:], ny[:], nt[:]):
                    chain(ins)
                chain(dve.tensor_tensor(ny[:], ny[:], lim[:], ALU.min))
                rn = rnorm4[:, bass.DynSlice(b.index(), 1), :].to_broadcast([P, SC * H, IP])
                chain(dve.tensor_tensor(fu[:].rearrange("p s h n -> p (s h) n"),
                                        ast[:].rearrange("p s h n -> p (s h) n"), rn, ALU.mult))
                nyb = ny[:].rearrange("p s h -> p (s h)").unsqueeze(2).to_broadcast([P, SC * H, IP])
                fuv = fu[:].rearrange("p s h n -> p (s h) n")
                chain(dve.tensor_tensor(fuv, fuv, nyb, ALU.mult))
                chain(dve.tensor_tensor(fu[:], fu[:], sip[:], ALU.add))
                fmv = fm[:].rearrange("p s h -> p (s h)")
                fmb = fmv.unsqueeze(2).to_broadcast([P, SC * H, IP])
                chain(dve.tensor_reduce(fmv, fuv, AX_X, ALU.max))
                chain(dve.tensor_tensor(fuv, fuv, fmb, ALU.subtract))
                b.reached(dve, s_fe, 1, 1)
                chain(dve.tensor_reduce(fmv, fuv, AX_X, ALU.add))
                chain(dve.reciprocal(fm[:], fm[:]))
                chain(dve.tensor_tensor(fm[:], fm[:], mask_sb[:].unsqueeze(2).to_broadcast([P, SC, H]), ALU.mult))
                chain(dve.tensor_tensor(pip[:].rearrange("p s h n -> p (s h) n"), fuv, fmb, ALU.mult))
                assert count[0] == SEMD, count[0]
                wait_fill(dve, l, b, "x2", before=True)
                b.reached(dve, s_rd[1], 1, 1)
                dve.tensor_tensor(at[1][:, :, 0:C].rearrange("p s (h d) -> p s h d", d=D), ust[:, :, :, 0:D],
                                  rd[1][:].unsqueeze(3).to_broadcast([P, SC, H, D]),
                                  ALU.mult).then_inc(s_at0, 1)

            def attend_ip(l, b, s):
                wait_fill(dve, l, b, f"ip{s}")
                b.reached(dve, s_at0, 1, 1)
                dve.tensor_tensor(at[1][:, s, 0:C], bank(l, f"ip{s}")[:, 0:C], at[1][:, s, 0:C], ALU.add)\
                   .then_inc(free_sem(l, f"ip{s}"), 1)

            def project(l, b, c):
                m = CC[c][1]
                wait_fill(dve, l, b, f"o{c}")
                b.reached(dve, s_res[l], 3, 3)
                o = bank(l, f"o{c}")[0:m, 0:S]
                if l == 0:
                    wait_fill(dve, 1, Batch(b.i, b.off - 1), "q2")
                    Batch(b.i, b.off - 1).reached(dve, s_res[1], 3, 3)
                    dve.tensor_tensor(xin[1][0:m, c, :], o, res[0][0:m, c, :], ALU.add)\
                       .then_inc(free_sem(l, f"o{c}"), 1)
                else:
                    b.reached(dve, s_store, 32, 0)
                    dve.tensor_tensor(outt[0:m, c, :], o, res[1][0:m, c, :], ALU.add)\
                       .then_inc(free_sem(l, f"o{c}"), 1)

            program(dve, {"v": values, "g": gram, "kt": turn_keys, "q": query, "s": scores, "m": turn_max,
                          "t": turned_scores, "a": attend, "sem": semantic, "ip": attend_ip, "o": project})

        @block.gpsimd
        def _(pool):
            pool.wait_ge(s_w, 16 * WEIGHTS)

            def blocks(l, b, n):
                hm = headmask[:].unsqueeze(1).unsqueeze(3)
                wait_fill(pool, l, b, f"t{NP - 1}", before=True)
                for k, (src, dst) in enumerate(((kh[l], kbh[l]), (kl[l], kbl[l]))):
                    if k == 0:
                        b.reached(pool, s_kh[l], 1, 1)
                    else:
                        wait_read(pool, l, b, "kt")
                    out4 = dst[:].rearrange("p (g h) t -> p g h t", h=GH)
                    pool.tensor_tensor(out4[:, :, :, 0:TXT[l]],
                                       src[:, :, 0:TXT[l]].unsqueeze(2).to_broadcast([P, G, GH, TXT[l]]),
                                       hm.to_broadcast([P, G, GH, TXT[l]]), ALU.mult).then_inc(s_kb[l], 1)
                    if l:
                        ki = (kih, kil)[k][:, bass.DynSlice(b.index(), 1), :, :].rearrange("p a g n -> p (a g) n")
                        pool.tensor_tensor(out4[:, :, :, TXT[1]:], ki.unsqueeze(2).to_broadcast([P, G, GH, IP]),
                                           hm.to_broadcast([P, G, GH, IP]), ALU.mult).then_inc(s_kb[l], 1)

            def residual(l, b, c):
                m = CC[c][1]
                if l == 0:
                    b.reached(pool, s_x, 32, 32)
                    wait_read(pool, 0, b, "o2", before=True)
                else:
                    wait_read(pool, 0, b, "o2")
                    wait_read(pool, 1, b, "o2", before=True)
                pool.tensor_tensor(res[l][0:m, c, :], xin[l][0:m, c, :], bias_sb[l][0:m, c:c + 1].to_broadcast([m, S]),
                                   ALU.add).then_inc(s_res[l], 1)

            def ip_values(l, b, n):
                b.reached(pool, s_viprow, 16 * H, 16 * H)
                wait_fill(pool, l, b, "ip1", before=True)
                pool.tensor_tensor(vbip[:].rearrange("k (h d) -> k h d", d=D),
                                   viprow[:].rearrange("k (h d) -> k h d", d=D),
                                   ipmask[:].unsqueeze(2).to_broadcast([H * IP, H, D]), ALU.mult).then_inc(s_vb, 1)

            program(pool, {"kt": blocks, "q": residual, "g": ip_values})


_OUT = (B, C, S)


def kernel(x, ctx_2048, fside_S_0, L0_xattn_Wq, L0_xattn_Wk, L0_xattn_Wv, L0_xattn_Wk_ip, L0_xattn_Wv_ip, L0_xattn_Wo,
           L0_xattn_bo, L1_xattn_W_q, L1_xattn_W_k, L1_xattn_W_v, L1_xattn_W_k_ip, L1_xattn_W_v_ip, L1_xattn_W_out,
           L1_xattn_b_out):
    from concourse import bacc
    from concourse.bass_utils import run_bass_kernel_spmd

    def turned(a):
        return np.ascontiguousarray(np.swapaxes(np.asarray(a), -1, -2))

    ctxt = turned(ctx_2048)
    row = np.arange(P) % HALF // D
    heads = np.arange(H)
    ind = np.zeros((P, H, T), np.float16)
    ind[heads, heads] = 1
    ind[32 + heads, heads] = 1
    arrays = {
        "x": turned(x), "ctx": ctxt,
        "ctxip": np.ascontiguousarray(np.moveaxis(ctxt[:, :, TXT[1]:], 1, 0)).reshape(E, B * IP),
        "mask": np.ascontiguousarray(np.asarray(fside_S_0).reshape(SC, P).T),
        "wq0": turned(L0_xattn_Wq), "wq1": np.asarray(L1_xattn_W_q),
        "wk0": turned(L0_xattn_Wk), "wk1": np.asarray(L1_xattn_W_k),
        "wv0": turned(L0_xattn_Wv), "wv1": np.asarray(L1_xattn_W_v),
        "wo0": turned(L0_xattn_Wo), "wo1": np.asarray(L1_xattn_W_out),
        "bias0": np.asarray(L0_xattn_bo).reshape(C, 1), "bias1": np.asarray(L1_xattn_b_out).reshape(C, 1),
        "wk_ip": np.repeat(np.asarray(L1_xattn_W_k_ip).reshape(E, G, 1, HALF), 2, axis=2).reshape(E, 2 * C), "wv_ip": np.asarray(L1_xattn_W_v_ip),
        "ident": np.eye(P, dtype=np.float32),
        "headmask": (row[:, None] == np.arange(GH)).astype(np.float16),
        "ipmask": (np.arange(H * IP)[:, None] // IP == heads).astype(np.float32),
        "ind": ind.reshape(P, H * T),
    }
    nc = bacc.Bacc("TRN2", target_bir_lowering=False, num_devices=1)
    ap = {n: nc.dram_tensor(f"in_{n}", a.shape, mybir.dt.from_np(a.dtype), kind="ExternalInput").ap()
          for n, a in arrays.items()}
    out = nc.dram_tensor("out", _OUT, F32, kind="ExternalOutput").ap()
    attention_stack_kernel(
        nc, ap["x"], ap["ctx"], ap["ctxip"], ap["mask"], (ap["wq0"], ap["wq1"]), (ap["wk0"], ap["wk1"]),
        (ap["wv0"], ap["wv1"]), (ap["wo0"], ap["wo1"]), (ap["bias0"], ap["bias1"]), ap["wk_ip"], ap["wv_ip"],
        ap["ident"], ap["headmask"], ap["ipmask"], ap["ind"], out)
    r = run_bass_kernel_spmd(nc, [{f"in_{n}": a for n, a in arrays.items()}], core_ids=[0])
    return turned(r.results[0]["out"])
```

```python
from contextlib import ExitStack

import numpy as np

import concourse.bass as bass
from concourse import mybir

F32 = mybir.dt.float32
F16 = mybir.dt.float16
I32 = mybir.dt.int32
ACT = mybir.ActivationFunctionType
ALU = mybir.AluOpType
AX_X = mybir.AxisListType.X

P = 128
B, S, C = 64, 256, 320
E = 512
H = 20
D = C // H
T = 77
IP = 4
TXT = (T, T - IP)
GH = 4
G = H // GH
HALF = GH * D
SC = S // P
EC = E // P
CC = [(0, 128), (128, 128), (256, 64)]
PAIR = 2
NP = H // PAIR
EF = 4
VW = (D + 1, D + 1 + T)
QH = 5
NQ = H // QH
AV = (SC, SC * NQ)
SM = float(D) ** -0.5
EPS = 1e-12
GS = 1.0 / 64
WS = 64.0
RING = 8
MAGIC = 0x5F3759DF
NEWTON = 3

CB = 8
CT = CB * T
HB = CB // 2
HT = HB * T
VT = [(k, min(P, CT - k)) for k in range(0, CT, P)]
KV_USES = ([("k", l, c, half) for l in (0, 1) for c in range(len(CC)) for half in (0, 1)]
           + [("v", l, k, 0) for l in (0, 1) for k in range(len(VT))] + [("g", 1, 0, half) for half in (0, 1)])
KU = len(KV_USES)
KV_STORES = 2 * len(CC) + 2 * 2 + 1


def pool_takes(layer, pair):
    return layer == 0 or pair % 2 == 1


class Batch:

    def __init__(self, i, off=0):
        self.i, self.off = i, off
        self.fixed = isinstance(i, int)

    def at(self, each, k):
        if each == 1:
            return self.i + (self.off + k)
        return self.i * each + (self.off * each + k)

    def index(self):
        return self.i + self.off

    def reached(self, eng, sem, each, k):
        if self.fixed and self.at(each, k) <= 0:
            return
        eng.wait_ge(sem, self.at(each, k))


AHEAD = ({"xh": 1, "xl": 1, "q": 1, "s": 1, "m": 1, "v": 1, "res": 1, "t": 0, "a": 0, "x": 0, "o": 0},
         {"xh": 0, "xl": -1, "q": -1, "s": -1, "m": -1, "v": -1, "g": -1, "vb": -1, "res": -1, "t": -1,
          "a": -2, "sem": -2, "fx": -2, "ks": -2, "at": -2, "pt": -2, "ip": -2, "x": -2, "o": -2})

ORDER = {
    "pe": """
        0t0 1a0 0t1 1a1 1a2 1a3 0t2 0t3 1q0 0t4 1a4 1a5 1q1 0t5 1q2 1a6 0t6 1a7 0t7 0t8 1s0 0t9 1s1 1s2 1s3 1s4 0q0
        0q1 0q2 1s5 0a0 0a1 1s6 0x0 0x1 0x2 1s7 1pt0 1s8 1s9 0o0 1m0 1ip0 1ip1 0o1 0o2 1t0 0s0 0s1 1x0 0s2 1t1 0s3
        1t2 0s4 1x1 1t3 0s5 1t4 0s6 1x2 0s7 0s8 1t5 1t6 1t7 0s9 1o0 1t8 1o1 0m0 1o2 1t9""",
    "act": """
        1a0 0t0 1a1 0t1 1a2 0t2 1a3 0t3 1q0 1a4 0t4 1a5 1q1 0t5 1q2 1a6 1a7 0t6 0t7 0t8 0t9 1s0 1s1 0q0 1s2 0q1 1s3
        1fx0 1s4 0q2 1s5 0x0 0x1 0x2 1s6 1pt0 1s7 1s8 1m0 1s9 1t0 1t1 1x0 1t2 1x1 1t3 1x2 1t4 1t5 1t6 1t7 1t8 0m0
        1t9""",
    "dve": """
        1a0 1a1 1a2 1a3 1q0 1a4 1a5 1q1 1q2 1a6 1a7 1sem0 1s0 1sem1 1s1 1sem2 1s2 1sem3 0q0 1s3 1sem4 1s4 0a0 0q1
        0q2 1s5 0a1 1sem5 1s6 0x0 0x1 0x2 1s7 1s8 1s9 1m0 0o0 1ip0 1ip1 0o1 1g0 0o2 0s0 0s1 1x0 0s2 1t0 0s3 0s4 1x1
        1t2 0s5 0s6 1x2 0s7 1xh0 1t4 0s8 0s9 1t6 1o0 0m0 1t8 1o1 1o2""",
    "pool": """
        1ks0 1xl0 0t0 0t1 1res0 0t2 0t3 0t4 1res1 1res2 0xh0 0t5 0xl0 0t6 0t7 0t8 0t9 1at0 1v0 1t1 0v0 1vb0 1t3
        0res0 1t5 0res1 1t7 0res2 1t9""",
}


def steps_of(engine):
    out = []
    for word in ORDER[engine].split():
        name = word[1:].rstrip("0123456789")
        out.append((int(word[0]), AHEAD[int(word[0])][name], name, int(word[1 + len(name):])))
    return out


FIRST_ALIKE = 3


class Ring:

    def __init__(self):
        used = steps_of("pe")
        self.on = [used[r::RING] for r in range(RING)]
        self.of = {(l, f"{name}{n}"): (k % RING, k // RING, off) for k, (l, off, name, n) in enumerate(used)}

    def bank(self, layer, use):
        return self.of[layer, use][0]

    def order(self, layer, use):
        r, k, off = self.of[layer, use]
        return k - off * len(self.on[r])

    def done(self, r, turn, k):
        def there(t, steps):
            return sum(0 <= t + off < B for _, off, _, _ in steps)
        return sum(there(t, self.on[r]) for t in range(-1, turn)) + there(turn, self.on[r][:k])

    def wait(self, eng, sems, b, layer, use, more):
        r, k, off = self.of[layer, use]
        shift = b.off - off
        if b.fixed:
            if 0 <= b.i + b.off and self.done(r, b.i + shift, k) + more > 0:
                eng.wait_ge(sems[r], self.done(r, b.i + shift, k) + more)
            return
        assert shift in (0, -1)
        each = len(self.on[r])
        eng.wait_ge(sems[r], b.i * each + ((shift - FIRST_ALIKE) * each + self.done(r, FIRST_ALIKE, k) + more))


def inverse_root(eng, done, sq, y, t):
    done(eng.tensor_scalar(y.bitcast(I32), sq.bitcast(I32), 1, None, ALU.logical_shift_right))
    done(eng.tensor_scalar(y.bitcast(I32), y.bitcast(I32), -1.0, float(MAGIC), ALU.mult, ALU.add))
    for _ in range(NEWTON):
        done(eng.tensor_tensor(t, y, y, ALU.mult))
        done(eng.scalar_tensor_tensor(t, t, -0.5, sq, ALU.mult, ALU.mult))
        done(eng.scalar_tensor_tensor(y, t, 1.5, y, ALU.add, ALU.mult))


def keys_and_values(nc, psum, ctx, ctxip, wk, wv, wq, wo, wk_ip, wv_ip, k_dram, v_dram, g_dram, vip_dram, wqs, wos,
                    rnorm4):
    both = (0, 1)
    PAIRS = B // CB // 2
    with ExitStack() as stack:
        def sb(name, shape, dt=F32):
            return stack.enter_context(nc.sbuf_tensor(name, shape, dt))

        def sem(name):
            return stack.enter_context(nc.semaphore(name))

        raw = {}
        split = {}
        for name in ("k0", "v0", "k1", "v1", "ki"):
            raw[name] = sb(f"raw_{name}", [P, EC, C])
            split[name] = sb(f"split_{name}", [P, 2, EC, C], F16)
        for l in both:
            for name, t in ((f"q{l}", wqs[l]), (f"o{l}", wos[l])):
                raw[name] = sb(f"raw_{name}", [P, 3, C])
                split[name] = t
        order = ["k0", "k1", "ki", "v0", "v1", "q0", "o0", "q1", "o1"]
        wvi = sb("wvi", [P, EC, C])
        ones = sb("ones", [P, P])
        one = sb("one", [P, EC])
        ctxip_sb = sb("ctxip_sb", [P, EC, B * IP])
        ipsq = sb("ipsq", [P, EC, B * IP])
        ipss = sb("ipss", [P, B * IP])
        ipy = sb("ipy", [P, B * IP])
        ipt = sb("ipt", [P, B * IP])
        vip = sb("vip", [P, 2, C])
        cx = sb("cx", [P, 2, EC, CT])
        ch = sb("ch", [P, 2, EC, CT], F16)
        cl = sb("cl", [P, 2, EC, CT], F16)
        kst = [sb(f"kst{l}", [P, 2, 3, 2, CT], F16) for l in both]
        vst = [sb(f"vst{l}", [P, 2, len(VT), 2, C], F16) for l in both]
        gst = sb("gst", [P, 2, CB, 2, T], F16)

        s_raw = {name: sem(f"raw_{name}_loaded") for name in order}
        s_ip = sem("ip_loaded")
        s_zero = sem("tails_cleared")
        s_wh, s_wl = sem("weights_high"), sem("weights_low")
        s_ctx = [sem(f"context_loaded{slot}") for slot in (0, 1)]
        s_ch, s_cl = sem("context_high"), sem("context_low")
        s_filled, s_high, s_freed = sem("kv_filled"), sem("kv_high"), sem("kv_freed")
        s_stored = [sem(f"kv_stored{slot}") for slot in (0, 1)]
        s_ipsq, s_ipf, s_vip, s_chain = sem("ip_squares"), sem("ip_filled"), sem("vip_read"), sem("ip_chain")
        s_last = sem("vip_stored")

        def pairs(eng, chunk):
            for slot in (0, 1):
                chunk(Batch(0), slot)
            with eng.Fori(1, PAIRS) as i:
                for slot in (0, 1):
                    chunk(Batch(i), slot)

        block = stack.enter_context(nc.Block())

        @block.sync
        def _(sp):
            def load_weight(name, src):
                if name[0] in "kv":
                    sp.dma_start(raw[name][:], src.rearrange("(k p) n -> p k n", p=P)).then_inc(s_raw[name], 16)
                else:
                    sp.dma_start(raw[name][:, 0:2, :], src[0:256, :].rearrange("(k p) n -> p k n", p=P))\
                      .then_inc(s_raw[name], 16)
                    sp.dma_start(raw[name][0:64, 2, :], src[256:320, :]).then_inc(s_raw[name], 16)

            def load_context(b, slot):
                src = ctx[:, bass.DynSlice(b.at(2 * CT, slot * CT), CT)].rearrange("(k p) n -> p k n", p=P)
                b.reached(sp, s_cl, 2, slot + 1 - 2)
                sp.dma_start(cx[:, slot, :, :], src).then_inc(s_ctx[slot], 16)

            def store(b, slot):
                batch = b.at(2 * CB, slot * CB)
                token = b.at(2 * CT, slot * CT)
                b.reached(sp, s_freed, 2 * KU, (slot + 1) * KU)
                for l in both:
                    for c, (c0, m) in reversed(list(enumerate(CC))):
                        dst = k_dram[l][:, c0:c0 + m, bass.DynSlice(token, CT)].rearrange("h c n -> c h n")
                        sp.dma_start(dst, kst[l][0:m, slot, c, :, :]).then_inc(s_stored[slot], 16)
                    full = len(VT) - 1
                    dst = v_dram[l][bass.DynSlice(token, full * P), :].rearrange("(k p) n -> p k n", p=P)
                    sp.dma_start(dst, vst[l][:, slot, 0:full, :, :].rearrange("p k h n -> p k (h n)"))\
                      .then_inc(s_stored[slot], 16)
                    dst = v_dram[l][bass.DynSlice(token + full * P, VT[-1][1]), :]
                    sp.dma_start(dst, vst[l][0:VT[-1][1], slot, full, :, :].rearrange("p h n -> p (h n)"))\
                      .then_inc(s_stored[slot], 16)
                dst = g_dram[bass.DynSlice(batch, CB), :, :].rearrange("b t n -> t b n")
                sp.dma_start(dst, gst[0:TXT[1], slot, :, :, :].rearrange("t b h n -> t b (h n)")).then_inc(s_stored[slot], 16)

            source = {"k0": wk[0], "k1": wk[1], "ki": wk_ip, "v0": wv[0], "v1": wv[1], "q0": wq[0], "q1": wq[1],
                      "o0": wo[0], "o1": wo[1]}
            load_weight("k0", source["k0"])
            load_context(Batch(0), 0)
            for name in order[1:5]:
                load_weight(name, source[name])
            load_context(Batch(0), 1)
            for name in order[5:]:
                load_weight(name, source[name])
            sp.dma_start(wvi[:], wv_ip.rearrange("(k p) n -> p k n", p=P)).then_inc(s_ip, 16)
            sp.dma_start(ctxip_sb[:], ctxip.rearrange("(k p) n -> p k n", p=P)).then_inc(s_ip, 16)
            for slot in (0, 1):
                load_context(Batch(1), slot)
            for slot in (0, 1):
                store(Batch(0), slot)
            with sp.Fori(2, PAIRS) as i:
                for slot in (0, 1):
                    load_context(Batch(i), slot)
                for slot in (0, 1):
                    store(Batch(i, -1), slot)
            for slot in (0, 1):
                store(Batch(PAIRS - 1), slot)
            sp.wait_ge(s_vip, 2)
            for k in range(2):
                sp.dma_start(vip_dram[k * P:(k + 1) * P, :], vip[:, k, :]).then_inc(s_last, 16)
            sp.wait_ge(s_last, 32)
            for slot in (0, 1):
                sp.wait_ge(s_stored[slot], 16 * KV_STORES * PAIRS)

        @block.tensor
        def _(pe):
            def three(out, parts):
                for n, (a, b) in enumerate(parts):
                    mm = pe.matmul(out, a, b, start=(n == 0), stop=(n == len(parts) - 1))
                return mm

            def products(wname, c0, m, rhs):
                w = split[wname]
                return [(w[:, hw, k, c0:c0 + m], rhs(hc, k)) for k in range(EC) for hw, hc in ((0, 0), (1, 0), (0, 1))]

            def chunk(b, slot):
                b.reached(pe, s_cl, 2, slot + 1)
                parts = (ch, cl)
                for u, (kind, l, c, half) in enumerate(KV_USES):
                    b.reached(pe, s_freed, 2 * KU, slot * KU + u + 1 - RING)
                    if b.fixed and slot == 0 and kind != "g":
                        pe.wait_ge(s_wl, {"k": (1, 3), "v": (4, 5)}[kind][l])
                    r = u % RING
                    cols = slice(half * HT, (half + 1) * HT)
                    if kind == "k":
                        c0, m = CC[c]
                        o = psum[0:m, r, 0:HT].rearrange("p (b t) -> p b t", t=T)

                        def tokens(t0, t1):
                            def of(h, k):
                                return parts[h][:, slot, k, cols].rearrange("p (b t) -> p b t", t=T)[:, :, t0:t1]
                            return of
                        mm = three(o[:, :, 0:TXT[l]], products(f"k{l}", c0, m, tokens(0, TXT[l])))
                        if l:
                            mm = three(o[:, :, TXT[1]:], products("ki", c0, m, tokens(TXT[1], T)))
                    elif kind == "v":
                        k0, m = VT[c]
                        w = split[f"v{l}"]
                        mm = three(psum[0:m, r, 0:C],
                                   [(parts[hc][:, slot, k, k0:k0 + m], w[:, hw, k, :])
                                    for k in range(EC) for hc, hw in ((0, 0), (0, 1), (1, 0))])
                    else:
                        for j in range(HB):
                            t0 = half * HT + j * T
                            mm = three(psum[0:TXT[1], r, j * T:(j + 1) * T],
                                       [(parts[h1][:, slot, k, t0:t0 + TXT[1]], parts[h2][:, slot, k, t0:t0 + T])
                                        for k in range(EC) for h1, h2 in ((0, 0), (0, 1), (1, 0))])
                    mm.then_inc(s_filled, 1)

            pairs(pe, chunk)
            pe.wait_ge(s_freed, KU * (B // CB))
            pe.wait_ge(s_ipsq, 2)
            pe.wait_ge(s_ip, 32)
            for j in range(2):
                for k in range(EC):
                    mm = pe.matmul(psum[:, j, 0:C], ctxip_sb[:, k, j * P:(j + 1) * P], wvi[:, k, :],
                                   start=(k == 0), stop=(k == EC - 1))
                mm.then_inc(s_ipf, 1)
            for k in range(EC):
                mm = pe.matmul(psum[:, 2, 0:B * IP], ones[:], ipsq[:, k, :], start=(k == 0), stop=(k == EC - 1))
            mm.then_inc(s_ipf, 1)

        def result(kind, l, c, half, slot):
            if kind == "k":
                m = CC[c][1]
                return [kst[l][0:m, slot, c, h, half * HT:(half + 1) * HT] for h in both], m, HT, 1 / WS
            if kind == "v":
                m = VT[c][1]
                return [vst[l][0:m, slot, c, h, :] for h in both], m, C, 1 / WS
            return [gst[0:TXT[1], slot, half * HB:(half + 1) * HB, h, :] for h in both], TXT[1], HT, GS

        def source_of(kind, m, n, u):
            o = psum[0:m, u % RING, 0:n]
            return o.rearrange("p (b t) -> p b t", t=T) if kind == "g" else o

        @block.scalar
        def _(act):
            for n, name in enumerate(order):
                act.wait_ge(s_raw[name], 16 if name[0] in "kv" else 32)
                if name == "q0":
                    act.wait_ge(s_zero, 4)
                t = split[name]
                act.activation(t[:, 0, :, :], raw[name][:], ACT.Copy, scale=WS).then_inc(s_wh, 1)

            def chunk(b, slot):
                b.reached(act, s_stored[slot], 16 * KV_STORES, 0)
                for u, (kind, l, c, half) in enumerate(KV_USES):
                    (high, _), m, n, scale = result(kind, l, c, half, slot)
                    b.reached(act, s_filled, 2 * KU, slot * KU + u + 1)
                    act.activation(high, source_of(kind, m, n, u), ACT.Copy, scale=scale).then_inc(s_high, 1)

            pairs(act, chunk)
            for j in range(2):
                act.wait_ge(s_ipf, j + 1)
                act.activation(vip[:, j, :], psum[:, j, 0:C], ACT.Copy).then_inc(s_vip, 1)

        @block.vector
        def _(dve):
            for n, name in enumerate(order):
                dve.wait_ge(s_wh, n + 1)
                t = split[name]
                dve.scalar_tensor_tensor(t[:, 1, :, :], raw[name][:], WS, t[:, 0, :, :], ALU.mult, ALU.subtract)\
                   .then_inc(s_wl, 1)
            dve.memset(ones[:], 1.0).then_inc(s_ipsq, 1)

            def chunk(b, slot):
                for u, (kind, l, c, half) in enumerate(KV_USES):
                    (high, low), m, n, scale = result(kind, l, c, half, slot)
                    b.reached(dve, s_high, 2 * KU, slot * KU + u + 1)
                    dve.scalar_tensor_tensor(low, source_of(kind, m, n, u), scale, high, ALU.mult, ALU.subtract)\
                       .then_inc(s_freed, 1)

            pairs(dve, chunk)
            dve.wait_ge(s_ip, 32)
            dve.tensor_tensor(ipsq[:], ctxip_sb[:], ctxip_sb[:], ALU.mult).then_inc(s_ipsq, 1)
            count = [0]

            def done(ins):
                count[0] += 1
                ins.then_inc(s_chain, 1)
                dve.wait_ge(s_chain, count[0])
            dve.wait_ge(s_ipf, 3)
            done(dve.tensor_scalar(ipss[:], psum[:, 2, 0:B * IP], EPS * EPS, None, ALU.max))
            inverse_root(dve, done, ipss[:], ipy[:], ipt[:])
            done(dve.tensor_scalar(rnorm4[:].rearrange("p b n -> p (b n)"), ipy[:], 4.0, None, ALU.mult))

        @block.gpsimd
        def _(pool):
            for l in both:
                for name in (f"q{l}", f"o{l}"):
                    pool.memset(raw[name][64:P, 2, :], 0.0).then_inc(s_zero, 1)
            pool.wait_ge(s_zero, 4)
            pool.memset(one[:], 1.0).then_inc(s_zero, 1)
            pool.wait_ge(s_zero, 5)

            def chunk(b, slot):
                b.reached(pool, s_ctx[slot], 16, 16)
                b.reached(pool, s_filled, 2 * KU, (slot - 1) * KU)
                pool.tensor_tensor(ch[:, slot, :, :], cx[:, slot, :, :],
                                   one[:].unsqueeze(2).to_broadcast([P, EC, CT]), ALU.mult).then_inc(s_ch, 1)
                b.reached(pool, s_ch, 2, slot + 1)
                pool.tensor_tensor(cl[:, slot, :, :], cx[:, slot, :, :], ch[:, slot, :, :], ALU.subtract)\
                    .then_inc(s_cl, 1)

            pairs(pool, chunk)


def attention(nc, psum, x, mask, bias, ident_d, ipmask_d, ind_d, k_dram, v_dram, g_dram, vip_dram, wqs, wos, rnorm4,
              out):
    both = (0, 1)
    with ExitStack() as stack:
        def sb(name, shape, dt=F32):
            return stack.enter_context(nc.sbuf_tensor(name, shape, dt))

        def sem(name):
            return stack.enter_context(nc.semaphore(name))

        ring = Ring()

        ident = sb("ident", [P, P])
        one = sb("one16", [P, H])
        ident16 = sb("ident16", [P, P], F16)
        ipmask = sb("ipmask", [H * IP, H])
        mask_sb = sb("mask_sb", [P, SC])
        bias_sb = [sb(f"bias{l}", [P, 3]) for l in both]
        xin = [sb(f"x{l}", [P, 3, S]) for l in both]
        xs = [sb(f"xs{l}", [P, 2, 3, S], F16) for l in both]
        res = [sb(f"res{l}", [P, 3, S]) for l in both]
        res_next = sb("res_next", [P, 3, S])
        kb = [sb(f"kb{l}", [P, GH, 2, G, T], F16) for l in both]
        vst = [sb(f"values{l}", [T, 2, C], F16) for l in both]
        gst = sb("gram", [T, 2, T], F16)
        vh = [sb(f"vh{l}", [P, H, VW[l]], F16) for l in both]
        vl = [sb(f"vl{l}", [P, H, VW[l]], F16) for l in both]
        qs = [sb(f"qs{l}", [P, G, S], F16) for l in both]
        qm = [sb(f"qm{l}", [P, G, S], F16) for l in both]
        nm = sb("nm", [P, SC, H])
        mneg = [sb(f"mneg{l}", [P, SC, P], F16) for l in both]
        ef = [sb(f"ef{l}", [P, EF, PAIR * S]) for l in both]
        eh = [sb(f"eh{l}", [P, H, S], F16) for l in both]
        el = [sb(f"el{l}", [P, H, S], F16) for l in both]
        est = sb("est", [P, SC, H, TXT[1]])
        rd = [sb(f"rd{l}", [P, SC, H]) for l in both]
        at = [sb(f"at{l}", [P, SC, 3 * P]) for l in both]
        att = [sb(f"att{l}", [P, 2, 3, S], F16) for l in both]
        sip = sb("sip", [P, SC, H, IP])
        sip2 = sb("sip2", [P, SC, H, IP])
        ust = sb("ust", [P, SC, H, D + 1])
        ast = sb("ast", [P, SC, H, IP])
        pe_ = sb("pe_", [P, 2, QH, TXT[1]])
        n2 = sb("n2", [P, SC, H])
        ny = sb("ny", [P, SC, H])
        nt = sb("nt", [P, SC, H])
        lim = sb("lim", [P, SC, H])
        fu = sb("fu", [P, SC, H, IP])
        fm = sb("fm", [P, SC, H])
        pip = sb("pip", [P, SC, H, IP])
        pt = sb("pt", [H * IP, S])
        viprow = sb("viprow", [H * IP, C])
        vbip = sb("vbip", [H * IP, C])
        outt = sb("outt", [P, 3, S])

        def pair(name):
            return [sem(f"{name}{l}") for l in both]
        filled = [sem(f"filled_{r}") for r in range(RING)]
        freed = [sem(f"freed_{r}") for r in range(RING)]
        s_w = sem("constants_loaded")
        s_ind = sem("head_picks_loaded")
        s_zero_dve, s_zero_pool = sem("cleared_by_dve"), sem("cleared_by_pool")
        s_x = sem("x_loaded")
        s_kb, s_vst, s_gst = pair("key_blocks_loaded"), pair("values_loaded"), sem("gram_loaded")
        s_viprow = sem("vip_rows_loaded")
        s_store = sem("out_stored")
        s_moved = sem("residual1_moved")
        s_res = pair("residual_")
        s_xh, s_xl = pair("x_high"), pair("x_low")
        s_v, s_gr = pair("value_table"), sem("gram_spread")
        s_qh, s_qm = pair("q_high"), pair("q_copied")
        s_mr, s_mx = sem("maxima_rounded"), sem("maxima")
        s_ms = pair("maxima_spread")
        s_el = pair("exp_low_dve"), pair("exp_low_pool")
        s_rd = pair("den_inverse")
        s_sip, s_ast, s_n2 = sem("ip_scores"), sem("ip_products"), sem("square_norms")
        s_semd, s_fe, s_vb = sem("ip_softmax_steps"), sem("ip_exp"), sem("vip_blocks")
        s_pip = sem("ip_probabilities")
        s_at0 = sem("text_attended")
        s_sip2 = sem("ip_scores_kept")
        s_ath = pair("attended_high")
        SEMD = 14 + 3 * NEWTON
        KB_LOADS = 2 * GH

        def bank(l, use):
            return psum[:, ring.bank(l, use), :]

        def previous(b):
            return Batch(b.i, b.off - 1)

        def wait_fill(eng, l, b, use, before=False):
            ring.wait(eng, filled, previous(b) if before else b, l, use, 1)

        def wait_free(eng, l, b, use, reads=()):
            latest = {ring.bank(l, use): (ring.order(l, use), use, 0)}
            for other in reads:
                r, k = ring.bank(l, other), ring.order(l, other) + 1
                if r not in latest or latest[r][0] < k:
                    latest[r] = (k, other, 1)
            for _, other, more in latest.values():
                ring.wait(eng, freed, b, l, other, more)

        def fill_sem(l, use):
            return filled[ring.bank(l, use)]

        def wait_read(eng, l, b, use, before=False):
            ring.wait(eng, freed, previous(b) if before else b, l, use, 1)

        def free_sem(l, use):
            return freed[ring.bank(l, use)]

        def low_done(l, p):
            def mine(upto, on_pool):
                return sum(pool_takes(l, q) == on_pool for q in range(upto))
            on_pool = pool_takes(l, p)
            return s_el[on_pool][l], mine(NP, on_pool), mine(p + 1, on_pool)

        def low_parts(eng, l, b, p):
            n = TXT[l]
            wait_read(eng, l, b, f"t{p}")
            eng.tensor_tensor(el[l][0:n, p * PAIR:(p + 1) * PAIR, :],
                              ef[l][0:n, p % EF, :].rearrange("t (h s) -> t h s", s=S),
                              eh[l][0:n, p * PAIR:(p + 1) * PAIR, :], ALU.subtract).then_inc(low_done(l, p)[0], 1)

        def turns(eng, turn):
            for i in range(-1, FIRST_ALIKE):
                turn(i)
            with eng.Fori(FIRST_ALIKE, B - 1) as i:
                turn(i)
            for i in range(B - 1, B + 2):
                turn(i)

        def program(eng, order, steps):
            def turn(i):
                for layer, off, name, n in order:
                    if not isinstance(i, int) or 0 <= i + off < B:
                        steps[name](layer, Batch(i, off), n)
            turns(eng, turn)

        dve_clears = [kb[0], kb[1], mneg[0], vh[0], vl[0], eh[0], el[0], vh[1], vl[1], mneg[1]]
        pool_clears = [xin[0], xin[1], at[0], at[1], eh[1], el[1]]
        DVE_CLEARS = len(dve_clears) + 3
        POOL_CLEARS = len(pool_clears) + 1
        WEIGHTS = 9
        block = stack.enter_context(nc.Block())

        @block.sync
        def _(sp):
            n = 0
            for t, d in [(ident, ident_d), (ipmask, ipmask_d), (mask_sb, mask)]:
                sp.dma_start(t[:], d).then_inc(s_w, 16)
                n += 1
            for l in both:
                for c, (c0, m) in enumerate(CC):
                    sp.dma_start(bias_sb[l][0:m, c:c + 1], bias[l][c0:c0 + m, :]).then_inc(s_w, 16)
                    n += 1
            assert n == WEIGHTS

            def load_x(b):
                b.reached(sp, s_xl[0], 1, 0)
                b.reached(sp, s_res[0], 3, 0)
                src = x[bass.DynSlice(b.index(), 1), :, :].rearrange("a c s -> (a c) s")
                sp.dma_start(xin[0][:, 0:2, :], src[0:256, :].rearrange("(k p) s -> p k s", p=P)).then_inc(s_x, 16)
                sp.dma_start(xin[0][0:64, 2, :], src[256:320, :]).then_inc(s_x, 16)

            def load_keys(l, b):
                src = k_dram[l].rearrange("h (g j d) n -> j d (h g) n", g=G, j=GH)
                tokens = bass.DynSlice(b.index() * T, T)
                wait_fill(sp, l, b, f"t{NP - 1}", before=True)
                for j in reversed(range(GH)):
                    for r, parts in ((0, 2), (1, 1)):
                        p0 = r * HALF + j * D
                        dst = kb[l][p0:p0 + D, j, 0:parts, :, :].rearrange("p h g t -> p (h g) t")
                        sp.dma_start(dst, src[j, :, 0:parts * G, tokens]).then_inc(s_kb[l], 16)

            def load_values(l, b):
                src = v_dram[l][bass.DynSlice(b.index() * T, T), :]
                b.reached(sp, s_v[l], 2, 0)
                sp.dma_start(vst[l][:].rearrange("t h n -> t (h n)"), src).then_inc(s_vst[l], 16)

            def load_gram(b):
                b.reached(sp, s_gr, 2, 0)
                src = g_dram[bass.DynSlice(b.index(), 1), :, :].rearrange("b t n -> (b t) n")
                sp.dma_start(gst[0:TXT[1], :, :].rearrange("t h n -> t (h n)"), src).then_inc(s_gst, 16)

            def load_vip(b):
                b.reached(sp, s_vb, 1, 0)
                src = vip_dram[bass.DynSlice(b.index() * IP, IP), :]
                sp.dma_start(viprow[:], src.unsqueeze(0).to_broadcast([H, IP, C])).then_inc(s_viprow, 16)

            def move_residual(b):
                b.reached(sp, s_res[1], 3, 3)
                sp.dma_start(res[1][:, 0:2, :], res_next[:, 0:2, :]).then_inc(s_moved, 16)
                sp.dma_start(res[1][0:64, 2, :], res_next[0:64, 2, :]).then_inc(s_moved, 16)

            def store(b):
                wait_read(sp, 1, b, "o2")
                dst = out[bass.DynSlice(b.index(), 1), :, :].rearrange("a c s -> (a c) s")
                sp.dma_start(dst[0:256, :].rearrange("(k p) s -> p k s", p=P), outt[:, 0:2, :]).then_inc(s_store, 16)
                sp.dma_start(dst[256:320, :], outt[0:64, 2, :]).then_inc(s_store, 16)

            sp.wait_ge(s_zero_dve, 2)
            sp.wait_ge(s_zero_pool, 1)
            for l in both:
                sp.dma_start(kb[l][HALF:P, :, 1, :, :], ind_d.rearrange("p (j g t) -> p j g t", j=GH, g=G))\
                  .then_inc(s_ind, 16)

            def turn(i):
                def there(off):
                    return not isinstance(i, int) or 0 <= i + off < B
                if there(-1):
                    load_keys(1, Batch(i, -1))
                if there(1):
                    load_x(Batch(i, 1))
                    load_values(0, Batch(i, 1))
                if there(-1):
                    load_values(1, Batch(i, -1))
                    load_gram(Batch(i, -1))
                    load_vip(Batch(i, -1))
                if there(1):
                    load_keys(0, Batch(i, 1))
                if there(-2):
                    store(Batch(i, -2))
                if there(-1):
                    move_residual(Batch(i, -1))
            turns(sp, turn)
            sp.wait_ge(s_store, 32 * B)

        @block.tensor
        def _(pe):
            pe.wait_ge(s_w, 16 * WEIGHTS)
            pe.wait_ge(s_ind, 32)
            pe.wait_ge(s_zero_dve, DVE_CLEARS)
            pe.wait_ge(s_zero_pool, POOL_CLEARS)

            def project_split(o, w, c0, m, xparts):
                parts = [(w[0:kk, hw, k, c0:c0 + m], xparts[0:kk, hx, k, :])
                         for k, (_, kk) in enumerate(CC) for hw, hx in ((0, 0), (1, 0), (0, 1))]
                for n, (a, b) in enumerate(parts):
                    mm = pe.matmul(o, a, b, start=(n == 0), stop=(n == len(parts) - 1))
                return mm

            def query(l, b, c):
                c0, m = CC[c]
                wait_free(pe, l, b, f"q{c}")
                b.reached(pe, s_xl[l], 1, 1)
                project_split(bank(l, f"q{c}")[0:m, 0:S], wqs[l], c0, m, xs[l]).then_inc(fill_sem(l, f"q{c}"), 1)

            def scores(l, b, n):
                s, g = divmod(n, G)
                use = f"s{n}"
                wait_free(pe, l, b, use, [f"q{g // 2}"])
                b.reached(pe, s_kb[l], 16 * KB_LOADS, 16 * KB_LOADS)
                o = bank(l, use)[:, 0:GH * T].rearrange("p (h t) -> p h t", t=T)
                q = qs[l][:, g, s * P:(s + 1) * P]
                mm = pe.matmul(o, q, kb[l][:, :, 0, g, :], start=True, stop=(l == 0))
                if l:
                    mm = pe.matmul(o, q[0:HALF, :], kb[l][0:HALF, :, 1, g, :], start=False, stop=True)
                mm.then_inc(fill_sem(l, use), 1)

            def turn_max(l, b, n):
                wait_free(pe, l, b, "m0", [] if l else [f"s{k}" for k in range(SC * G)])
                if l:
                    b.reached(pe, s_mr, SC * G, SC * G)
                o = bank(l, "m0").bitcast(F16)
                for s in range(SC):
                    mm = pe.transpose(o[:, s * P:(s + 1) * P], mneg[l][:, s, :], ident16[:])
                mm.then_inc(fill_sem(l, "m0"), 1)

            def turned_scores(l, b, p):
                use = f"t{p}"
                wait_free(pe, l, b, use, ["m0"])
                b.reached(pe, s_qm[l], 1, 1)
                if p * PAIR >= GH:
                    b.reached(pe, s_ms[l], 1, 1)
                for j in range(PAIR):
                    g, hj = divmod(p * PAIR + j, GH)
                    o = bank(l, use)[0:TXT[l], j * S:(j + 1) * S]
                    pe.matmul(o, kb[l][:, hj, 0, g, 0:TXT[l]], qs[l][:, g, :], start=True, stop=False)
                    mm = pe.matmul(o, kb[l][:, hj, 1, g, 0:TXT[l]], qm[l][:, g, :], start=False, stop=True)
                mm.then_inc(fill_sem(l, use), 1)

            def attend(l, b, n):
                use = f"a{n}"
                s, q = divmod(n, NQ) if l else (n, 0)
                heads = range(q * QH, (q + 1) * QH) if l else range(H)
                wait_free(pe, l, b, use, [f"t{p}" for p in range(heads[0] // PAIR, heads[-1] // PAIR + 1)])
                last = heads[-1] // PAIR
                for on_pool in {pool_takes(l, p) for p in range(NP)}:
                    p = max(p for p in range(last + 1) if pool_takes(l, p) == on_pool)
                    b.reached(pe, *low_done(l, p))
                b.reached(pe, s_v[l], 2, 2)
                if l:
                    b.reached(pe, s_gr, 2, 2)
                w = VW[l]
                for k, h in enumerate(heads):
                    o = bank(l, use)[:, k * w:(k + 1) * w]
                    e_h, e_l = eh[l][:, h, s * P:(s + 1) * P], el[l][:, h, s * P:(s + 1) * P]
                    pe.matmul(o, e_h, vh[l][:, h, :], start=True, stop=False)
                    pe.matmul(o, e_h, vl[l][:, h, :], start=False, stop=False)
                    mm = pe.matmul(o, e_l, vh[l][:, h, :], start=False, stop=True)
                mm.then_inc(fill_sem(l, use), 1)

            def turn_probs(l, b, n):
                wait_free(pe, l, b, "pt0")
                b.reached(pe, s_pip, 1, 1)
                for s in range(SC):
                    mm = pe.transpose(bank(l, "pt0")[0:H * IP, s * P:(s + 1) * P],
                                      pip[:, s, :, :].rearrange("p h n -> p (h n)"), ident[:])
                mm.then_inc(fill_sem(l, "pt0"), 1)

            def attend_ip(l, b, s):
                use = f"ip{s}"
                wait_free(pe, l, b, use, ["pt0"])
                b.reached(pe, s_vb, 1, 1)
                pe.matmul(bank(l, use)[:, 0:C], pt[:, s * P:(s + 1) * P], vbip[:],
                          start=True, stop=True).then_inc(fill_sem(l, use), 1)

            def turn_attended(l, b, c):
                wait_free(pe, l, b, f"x{c}", [f"{'ip' if l else 'a'}{s}" for s in range(SC)])
                for s in range(SC):
                    mm = pe.transpose(bank(l, f"x{c}")[:, s * P:(s + 1) * P], at[l][:, s, c * P:(c + 1) * P], ident[:])
                mm.then_inc(fill_sem(l, f"x{c}"), 1)

            def project(l, b, c):
                c0, m = CC[c]
                wait_free(pe, l, b, f"o{c}", [f"x{k}" for k in range(3)])
                project_split(bank(l, f"o{c}")[0:m, 0:S], wos[l], c0, m, att[l]).then_inc(fill_sem(l, f"o{c}"), 1)

            program(pe, steps_of("pe"), {"q": query, "s": scores, "m": turn_max, "t": turned_scores, "a": attend, "pt": turn_probs,
                         "ip": attend_ip, "x": turn_attended, "o": project})

        @block.scalar
        def _(act):
            act.wait_ge(s_zero_dve, DVE_CLEARS)
            act.wait_ge(s_zero_pool, POOL_CLEARS)

            def query(l, b, c):
                wait_fill(act, l, b, f"q{c}")
                wait_fill(act, l, b, f"t{NP - 1}", before=True)
                for j in range(CC[c][1] // HALF):
                    act.activation(qs[l][0:HALF, 2 * c + j, :], bank(l, f"q{c}")[j * HALF:(j + 1) * HALF, 0:S],
                                   ACT.Copy, scale=SM / WS).then_inc(s_qh[l], 1)

            def scores(l, b, n):
                s, g = divmod(n, G)
                b.reached(act, s_mx, SC * G, n + 1)
                wait_read(act, 1, b, f"a{AV[1] - 1}", before=True)
                b.reached(act, s_sip2, 1, 0)
                o = bank(l, f"s{n}")[:, 0:GH * T].rearrange("p (h t) -> p h t", t=T)
                act.activation(sip[:, s, g * GH:(g + 1) * GH, :], o[:, :, TXT[1]:T], ACT.Copy).then_inc(s_sip, 1)
                for j in range(GH):
                    h = g * GH + j
                    ins = act.activation(est[:, s, h, :], o[:, j, 0:TXT[1]], ACT.Exp, bias=nm[:, s, h:h + 1])
                ins.then_inc(free_sem(l, f"s{n}"), 1)

            def turn_max(l, b, n):
                wait_fill(act, l, b, "m0")
                wait_fill(act, l, b, f"t{NP - 1}", before=True)
                act.activation(qm[l][HALF:P, 0, :], bank(l, "m0").bitcast(F16)[HALF:P, 0:S], ACT.Copy)\
                   .then_inc(free_sem(l, "m0"), 1)

            def turned_scores(l, b, p):
                use = f"t{p}"
                wait_fill(act, l, b, use)
                low, each, count = low_done(l, (p - EF) % NP)
                b.reached(act, low, each, count if p >= EF else count - each)
                n = TXT[l]
                act.activation(ef[l][0:n, p % EF, :], bank(l, use)[0:n, :], ACT.Exp)
                wait_fill(act, l, b, f"a{AV[l] - 1}", before=True)
                act.activation(eh[l][0:n, p * PAIR:(p + 1) * PAIR, :],
                               bank(l, use)[0:n, :].rearrange("t (h s) -> t h s", s=S), ACT.Exp)\
                   .then_inc(free_sem(l, use), 1)

            def attend(l, b, n):
                s, q = divmod(n, NQ)
                wait_fill(act, l, b, f"a{n}")
                b.reached(act, s_at0, 1, 0)
                o = bank(l, f"a{n}")[:, 0:QH * VW[1]].rearrange("p (h w) -> p h w", w=VW[1])
                act.activation(ust[:, s, q * QH:(q + 1) * QH, :], o[:, :, 0:D + 1], ACT.Copy)
                act.activation(ast[:, s, q * QH:(q + 1) * QH, :], o[:, :, D + 1 + TXT[1]:], ACT.Copy).then_inc(s_ast, 1)

            def fused_exp(l, b, n):
                b.reached(act, s_semd, SEMD, SEMD - 3)
                act.activation(fu[:], fu[:], ACT.Exp).then_inc(s_fe, 1)

            def turn_probs(l, b, n):
                wait_fill(act, l, b, "pt0")
                act.activation(pt[:], bank(l, "pt0")[0:H * IP, 0:S], ACT.Copy).then_inc(free_sem(l, "pt0"), 1)

            def turn_attended(l, b, c):
                m = CC[c][1]
                wait_fill(act, l, b, f"x{c}")
                act.activation(att[l][0:m, 0, c, :], bank(l, f"x{c}")[0:m, 0:S], ACT.Copy).then_inc(s_ath[l], 1)

            program(act, steps_of("act"), {"q": query, "s": scores, "m": turn_max, "t": turned_scores, "a": attend, "fx": fused_exp,
                          "pt": turn_probs, "x": turn_attended})

        @block.vector
        def _(dve):
            for t in dve_clears:
                dve.memset(t[:], 0.0).then_inc(s_zero_dve, 1)
            dve.wait_ge(s_zero_dve, len(dve_clears))
            for l in both:
                dve.memset(vh[l][0:TXT[l], :, D:D + 1], 1.0).then_inc(s_zero_dve, 1)
            dve.wait_ge(s_w, 16 * WEIGHTS)
            dve.tensor_copy(ident16[:], ident[:]).then_inc(s_zero_dve, 1)
            dve.wait_ge(s_zero_dve, DVE_CLEARS)
            dve.wait_ge(s_zero_pool, POOL_CLEARS)

            def high_input(l, b, n):
                for c in range(3):
                    wait_read(dve, 0, b, f"o{c}")
                wait_fill(dve, l, b, "q2", before=True)
                dve.tensor_copy(xs[l][:, 0, :, :], xin[l][:]).then_inc(s_xh[l], 1)

            def gram(l, b, n):
                b.reached(dve, s_gst, 16, 16)
                wait_fill(dve, l, b, f"a{AV[l] - 1}", before=True)
                for h, t in enumerate((vh[1], vl[1])):
                    dve.tensor_copy(t[0:TXT[1], :, D + 1:],
                                    gst[0:TXT[1], h, :].unsqueeze(1).to_broadcast([TXT[1], H, T])).then_inc(s_gr, 1)

            def query(l, b, c):
                groups = CC[c][1] // HALF
                for j in range(groups):
                    g = 2 * c + j
                    b.reached(dve, s_qh[l], G, g + 1)
                    ins = dve.scalar_tensor_tensor(qs[l][HALF:P, g, :], bank(l, f"q{c}")[j * HALF:(j + 1) * HALF, 0:S],
                                                   SM / WS, qs[l][0:HALF, g, :], ALU.mult, ALU.subtract)
                ins.then_inc(free_sem(l, f"q{c}"), 1)
                if c == 2:
                    wait_fill(dve, l, b, f"t{NP - 1}", before=True)
                    dve.tensor_copy(qm[l][0:HALF, :, :], qs[l][0:HALF, :, :]).then_inc(s_qm[l], 1)

            def scores(l, b, n):
                s, g = divmod(n, G)
                wait_fill(dve, l, b, f"s{n}")
                wait_fill(dve, l, b, "m0", before=True)
                o = bank(l, f"s{n}")[:, 0:GH * T].rearrange("p (h t) -> p h t", t=T)[:, :, 0:TXT[l]]
                m = mneg[l][:, s, HALF + g * GH:HALF + (g + 1) * GH]
                dve.tensor_reduce(m, o, AX_X, ALU.max, negate=True).then_inc(s_mr if l else free_sem(l, f"s{n}"), 1)
                if l:
                    wait_read(dve, l, b, f"s{n}", before=True)
                    b.reached(dve, s_mr, SC * G, n + 1)
                    dve.tensor_copy(nm[:, s, g * GH:(g + 1) * GH], m).then_inc(s_mx, 1)

            def turn_max(l, b, n):
                wait_read(dve, l, b, "m0")
                dve.tensor_copy(qm[l][HALF:P, 1:, :], qm[l][HALF:P, 0:1, :].to_broadcast([HALF, G - 1, S]))\
                   .then_inc(s_ms[l], 1)

            def turned_scores(l, b, p):
                low_parts(dve, l, b, p)

            def attend(l, b, n):
                if l == 0:
                    wait_fill(dve, l, b, f"a{n}")
                    o = bank(l, f"a{n}")[:, 0:H * VW[0]].rearrange("p (h w) -> p h w", w=VW[0])
                    wait_read(dve, l, b, f"a{n}", before=True)
                    dve.reciprocal(rd[0][:, n, :], o[:, :, D]).then_inc(s_rd[0], 1)
                    b.reached(dve, s_rd[0], SC, n + 1)
                    wait_fill(dve, l, b, "x2", before=True)
                    dve.tensor_tensor(at[0][:, n, 0:C].rearrange("p (h d) -> p h d", d=D), o[:, :, 0:D],
                                      rd[0][:, n, :].unsqueeze(2).to_broadcast([P, H, D]), ALU.mult)\
                       .then_inc(free_sem(l, f"a{n}"), 1)
                    return
                s, q = divmod(n, NQ)
                b.reached(dve, s_ast, SC * NQ, n + 1)
                b.reached(dve, s_n2, SC * NQ, n - 1)
                o = bank(l, f"a{n}")[:, 0:QH * VW[1]].rearrange("p (h w) -> p h w", w=VW[1])
                dve.tensor_tensor(pe_[:, n % 2, :, :], o[:, :, D + 1:D + 1 + TXT[1]], est[:, s, q * QH:(q + 1) * QH, :],
                                  ALU.mult).then_inc(free_sem(l, f"a{n}"), 1)
                wait_read(dve, l, b, f"a{n}")
                dve.tensor_reduce(n2[:, s, q * QH:(q + 1) * QH], pe_[:, n % 2, :, :], AX_X, ALU.add).then_inc(s_n2, 1)

            def semantic(l, b, n):
                def after(k):
                    b.reached(dve, s_semd, SEMD, k)

                den = ust[:, :, :, D]
                fuv = fu[:].rearrange("p s h n -> p (s h) n")
                fmv = fm[:].rearrange("p s h -> p (s h)")
                fmb = fmv.unsqueeze(2).to_broadcast([P, SC * H, IP])
                guess, newton = 4, 5
                last = newton + 3 * NEWTON
                if n == 0:
                    b.reached(dve, s_ast, SC * NQ, SC * NQ)
                    dve.tensor_scalar(lim[:], den, EPS / 8, None, ALU.mult).then_inc(s_semd, 1)
                    b.reached(dve, s_at0, 1, 0)
                    dve.reciprocal(rd[1][:], den).then_inc(s_rd[1], 1)
                    b.reached(dve, s_n2, SC * NQ, SC * NQ)
                    dve.tensor_scalar(n2[:], n2[:], 1e-37, None, ALU.max).then_inc(s_semd, 1)
                    after(1)
                    dve.reciprocal(lim[:], lim[:]).then_inc(s_semd, 1)
                    after(2)
                    dve.tensor_scalar(ny[:].bitcast(I32), n2[:].bitcast(I32), 1, None, ALU.logical_shift_right)\
                       .then_inc(s_semd, 1)
                    after(guess)
                    dve.tensor_scalar(ny[:].bitcast(I32), ny[:].bitcast(I32), -1.0, float(MAGIC), ALU.mult, ALU.add)\
                       .then_inc(s_semd, 1)
                elif n <= NEWTON:
                    first = newton + 3 * (n - 1)
                    after(first)
                    dve.tensor_tensor(nt[:], ny[:], ny[:], ALU.mult).then_inc(s_semd, 1)
                    after(first + 1)
                    dve.scalar_tensor_tensor(nt[:], nt[:], -0.5, n2[:], ALU.mult, ALU.mult).then_inc(s_semd, 1)
                    after(first + 2)
                    dve.scalar_tensor_tensor(ny[:], nt[:], 1.5, ny[:], ALU.add, ALU.mult).then_inc(s_semd, 1)
                elif n == NEWTON + 1:
                    rn = rnorm4[:, bass.DynSlice(b.index(), 1), :].to_broadcast([P, SC * H, IP])
                    dve.tensor_tensor(fuv, ast[:].rearrange("p s h n -> p (s h) n"), rn, ALU.mult).then_inc(s_semd, 1)
                    after(last)
                    dve.tensor_tensor(ny[:], ny[:], lim[:], ALU.min).then_inc(s_semd, 1)
                    after(last + 2)
                    nyb = ny[:].rearrange("p s h -> p (s h)").unsqueeze(2).to_broadcast([P, SC * H, IP])
                    dve.tensor_tensor(fuv, fuv, nyb, ALU.mult).then_inc(s_semd, 1)
                    after(last + 3)
                    b.reached(dve, s_sip2, 1, 1)
                    dve.tensor_tensor(fu[:], fu[:], sip2[:], ALU.add).then_inc(s_semd, 1)
                    after(last + 4)
                    dve.tensor_reduce(fmv, fuv, AX_X, ALU.max).then_inc(s_semd, 1)
                    after(last + 5)
                    dve.tensor_tensor(fuv, fuv, fmb, ALU.subtract).then_inc(s_semd, 1)
                else:
                    b.reached(dve, s_fe, 1, 1)
                    dve.tensor_reduce(fmv, fuv, AX_X, ALU.add).then_inc(s_semd, 1)
                    after(SEMD - 2)
                    dve.reciprocal(fm[:], fm[:]).then_inc(s_semd, 1)
                    after(SEMD - 1)
                    dve.tensor_tensor(fm[:], fm[:], mask_sb[:].unsqueeze(2).to_broadcast([P, SC, H]), ALU.mult)\
                       .then_inc(s_semd, 1)
                    wait_fill(dve, l, b, "pt0", before=True)
                    after(SEMD)
                    dve.tensor_tensor(pip[:].rearrange("p s h n -> p (s h) n"), fuv, fmb, ALU.mult).then_inc(s_pip, 1)

            def attend_ip(l, b, s):
                wait_fill(dve, l, b, f"ip{s}")
                b.reached(dve, s_at0, 1, 1)
                dve.tensor_tensor(at[1][:, s, 0:C], bank(l, f"ip{s}")[:, 0:C], at[1][:, s, 0:C], ALU.add)\
                   .then_inc(free_sem(l, f"ip{s}"), 1)

            def turn_attended(l, b, c):
                m = CC[c][1]
                b.reached(dve, s_ath[l], 3, c + 1)
                dve.tensor_tensor(att[l][0:m, 1, c, :], bank(l, f"x{c}")[0:m, 0:S], att[l][0:m, 0, c, :], ALU.subtract)\
                   .then_inc(free_sem(l, f"x{c}"), 1)

            def project(l, b, c):
                m = CC[c][1]
                wait_fill(dve, l, b, f"o{c}")
                o = bank(l, f"o{c}")[0:m, 0:S]
                if l == 0:
                    b.reached(dve, s_res[0], 3, 3)
                    previous(b).reached(dve, s_xl[1], 1, 1)
                    previous(b).reached(dve, s_res[1], 3, 3)
                    dst = xin[1][0:m, c, :]
                else:
                    b.reached(dve, s_moved, 32, 32)
                    b.reached(dve, s_store, 32, 0)
                    dst = outt[0:m, c, :]
                dve.scalar_tensor_tensor(dst, o, 1 / WS, res[l][0:m, c, :], ALU.mult, ALU.add)\
                   .then_inc(free_sem(l, f"o{c}"), 1)

            program(dve, steps_of("dve"), {"xh": high_input, "g": gram, "q": query, "s": scores, "m": turn_max, "t": turned_scores,
                          "a": attend, "sem": semantic, "ip": attend_ip, "x": turn_attended, "o": project})

        @block.gpsimd
        def _(pool):
            for t in pool_clears:
                pool.memset(t[:], 0.0).then_inc(s_zero_pool, 1)
            pool.memset(one[:], 1.0).then_inc(s_zero_pool, 1)
            pool.wait_ge(s_w, 16 * WEIGHTS)
            pool.wait_ge(s_zero_pool, POOL_CLEARS)
            pool.wait_ge(s_zero_dve, DVE_CLEARS)

            def high_input(l, b, n):
                b.reached(pool, s_x, 32, 32)
                wait_fill(pool, l, b, "q2", before=True)
                pool.tensor_tensor(xs[l][:, 0, :, :], xin[l][:], one[:, 0:1].unsqueeze(2).to_broadcast([P, 3, S]),
                                   ALU.mult).then_inc(s_xh[l], 1)

            def low_input(l, b, n):
                b.reached(pool, s_xh[l], 1, 1)
                pool.tensor_tensor(xs[l][:, 1, :, :], xin[l][:], xs[l][:, 0, :, :], ALU.subtract).then_inc(s_xl[l], 1)

            def values(l, b, n):
                b.reached(pool, s_vst[l], 16, 16)
                wait_fill(pool, l, b, f"a{AV[l] - 1}", before=True)
                m = TXT[l]
                for h, t in enumerate((vh[l], vl[l])):
                    pool.tensor_tensor(t[0:m, :, 0:D], vst[l][0:m, h, :].rearrange("t (h d) -> t h d", d=D),
                                       one[0:m, :].unsqueeze(2).to_broadcast([m, H, D]), ALU.mult).then_inc(s_v[l], 1)

            def residual(l, b, c):
                m = CC[c][1]
                if l == 0:
                    b.reached(pool, s_x, 32, 32)
                    wait_read(pool, 0, b, f"o{c}", before=True)
                    dst = res[0]
                else:
                    wait_read(pool, 0, b, f"o{c}")
                    b.reached(pool, s_moved, 32, 0)
                    dst = res_next
                pool.tensor_tensor(dst[0:m, c, :], xin[l][0:m, c, :], bias_sb[l][0:m, c:c + 1].to_broadcast([m, S]),
                                   ALU.add).then_inc(s_res[l], 1)

            def ip_values(l, b, n):
                b.reached(pool, s_viprow, 16, 16)
                wait_fill(pool, l, b, "ip1", before=True)
                pool.tensor_tensor(vbip[:].rearrange("k (h d) -> k h d", d=D),
                                   viprow[:].rearrange("k (h d) -> k h d", d=D),
                                   ipmask[:].unsqueeze(2).to_broadcast([H * IP, H, D]), ALU.mult).then_inc(s_vb, 1)

            def turned_scores(l, b, p):
                low_parts(pool, l, b, p)

            def keep_ip_scores(l, b, n):
                b.reached(pool, s_sip, SC * G, SC * G)
                b.reached(pool, s_semd, SEMD, 0)
                pool.tensor_tensor(sip2[:], sip[:], one[:].unsqueeze(1).unsqueeze(3).to_broadcast([P, SC, H, IP]),
                                   ALU.mult).then_inc(s_sip2, 1)

            def attended_text(l, b, n):
                wait_fill(pool, l, b, "x2", before=True)
                b.reached(pool, s_rd[1], 1, 1)
                pool.tensor_tensor(at[1][:, :, 0:C].rearrange("p s (h d) -> p s h d", d=D), ust[:, :, :, 0:D],
                                   rd[1][:].unsqueeze(3).to_broadcast([P, SC, H, D]), ALU.mult).then_inc(s_at0, 1)

            program(pool, steps_of("pool"), {"ks": keep_ip_scores, "at": attended_text, "xh": high_input, "xl": low_input, "v": values, "res": residual, "vb": ip_values, "t": turned_scores})


def attention_stack_kernel(nc, x, ctx, ctxip, mask, wq, wk, wv, wo, bias, wk_ip, wv_ip, ident_d, ipmask_d, ind_d, out):
    both = (0, 1)
    k_dram = [nc.dram_tensor(f"k_dram{l}", (2, C, B * T), F16, kind="Internal").ap() for l in both]
    v_dram = [nc.dram_tensor(f"v_dram{l}", (B * T, 2 * C), F16, kind="Internal").ap() for l in both]
    g_dram = nc.dram_tensor("g_dram", (B, TXT[1], 2 * T), F16, kind="Internal").ap()
    vip_dram = nc.dram_tensor("vip_dram", (B * IP, C), F32, kind="Internal").ap()
    with ExitStack() as stack:
        def sb(name, shape, dt=F32):
            return stack.enter_context(nc.sbuf_tensor(name, shape, dt))
        psum = stack.enter_context(nc.psum_tensor("psum", [P, RING, 512], F32))
        wqs = [sb(f"wq{l}", [P, 2, 3, C], F16) for l in both]
        wos = [sb(f"wo{l}", [P, 2, 3, C], F16) for l in both]
        rnorm4 = sb("rnorm4", [P, B, IP])
        keys_and_values(nc, psum, ctx, ctxip, wk, wv, wq, wo, wk_ip, wv_ip, k_dram, v_dram, g_dram, vip_dram, wqs, wos,
                        rnorm4)
        attention(nc, psum, x, mask, bias, ident_d, ipmask_d, ind_d, k_dram, v_dram, g_dram, vip_dram, wqs, wos, rnorm4,
                  out)


_OUT = (B, C, S)


def kernel(x, ctx_2048, fside_S_0, L0_xattn_Wq, L0_xattn_Wk, L0_xattn_Wv, L0_xattn_Wk_ip, L0_xattn_Wv_ip, L0_xattn_Wo,
           L0_xattn_bo, L1_xattn_W_q, L1_xattn_W_k, L1_xattn_W_v, L1_xattn_W_k_ip, L1_xattn_W_v_ip, L1_xattn_W_out,
           L1_xattn_b_out):
    from concourse import bacc
    from concourse.bass_utils import run_bass_kernel_spmd

    def turned(a):
        return np.ascontiguousarray(np.swapaxes(np.asarray(a), -1, -2))

    ctxt = np.moveaxis(np.asarray(ctx_2048), 2, 0)
    heads = np.arange(H)
    ind = np.zeros((HALF, GH, G, T), np.float16)
    ind[heads, heads % GH, heads // GH] = 1
    arrays = {
        "x": turned(x), "ctx": np.ascontiguousarray(ctxt).reshape(E, B * T),
        "ctxip": np.ascontiguousarray(ctxt[:, :, TXT[1]:]).reshape(E, B * IP),
        "mask": np.ascontiguousarray(np.asarray(fside_S_0).reshape(SC, P).T),
        "wq0": turned(L0_xattn_Wq), "wq1": np.asarray(L1_xattn_W_q),
        "wk0": turned(L0_xattn_Wk), "wk1": np.asarray(L1_xattn_W_k),
        "wv0": turned(L0_xattn_Wv), "wv1": np.asarray(L1_xattn_W_v),
        "wo0": turned(L0_xattn_Wo), "wo1": np.asarray(L1_xattn_W_out),
        "bias0": np.asarray(L0_xattn_bo).reshape(C, 1), "bias1": np.asarray(L1_xattn_b_out).reshape(C, 1),
        "wk_ip": np.asarray(L1_xattn_W_k_ip), "wv_ip": np.asarray(L1_xattn_W_v_ip),
        "ident": np.eye(P, dtype=np.float32),
        "ipmask": (np.arange(H * IP)[:, None] // IP == heads).astype(np.float32),
        "ind": ind.reshape(HALF, H * T),
    }
    nc = bacc.Bacc("TRN2", target_bir_lowering=False, num_devices=1)
    ap = {n: nc.dram_tensor(f"in_{n}", a.shape, mybir.dt.from_np(a.dtype), kind="ExternalInput").ap()
          for n, a in arrays.items()}
    out = nc.dram_tensor("out", _OUT, F32, kind="ExternalOutput").ap()
    attention_stack_kernel(
        nc, ap["x"], ap["ctx"], ap["ctxip"], ap["mask"], (ap["wq0"], ap["wq1"]), (ap["wk0"], ap["wk1"]),
        (ap["wv0"], ap["wv1"]), (ap["wo0"], ap["wo1"]), (ap["bias0"], ap["bias1"]), ap["wk_ip"], ap["wv_ip"],
        ap["ident"], ap["ipmask"], ap["ind"], out)
    r = run_bass_kernel_spmd(nc, [{f"in_{n}": a for n, a in arrays.items()}], core_ids=[0])
    return turned(r.results[0]["out"])
```

```python
from contextlib import ExitStack

import numpy as np

import concourse.bass as bass
from concourse import mybir

F32 = mybir.dt.float32
F16 = mybir.dt.float16
I32 = mybir.dt.int32
ACT = mybir.ActivationFunctionType
ALU = mybir.AluOpType
AX_X = mybir.AxisListType.X

P = 128
B, S, C = 64, 256, 320
E = 512
H = 20
D = C // H
T = 77
IP = 4
TXT = (T, T - IP)
GH = 4
G = H // GH
HALF = GH * D
SC = S // P
EC = E // P
CC = [(0, 128), (128, 128), (256, 64)]
PAIR = 2
NP = H // PAIR
EF = 4
VW = (D + 1, D + 1 + T)
QH = 5
NQ = H // QH
AV = (SC, SC * NQ)
SM = float(D) ** -0.5
EPS = 1e-12
GS = 1.0 / 64
WS = 64.0
RING = 8
MAGIC = 0x5F3759DF
NEWTON = 3

CB = 8
CT = CB * T
HB = CB // 2
HT = HB * T
VT = [(k, min(P, CT - k)) for k in range(0, CT, P)]
FULL, TAIL = len(CC) - 1, CC[-1][0]
KV_USES = ([("k", l, c, half) for l in (0, 1) for c in range(FULL) for half in (0, 1)]
           + [("kt", 0, 0, half) for half in (0, 1)] + [("ki", 1, 0, 0)]
           + [("g", 1, 0, half) for half in (0, 1)] + [("v", l, k, 0) for l in (0, 1) for k in range(len(VT))])
KU = len(KV_USES)
KV_STORES = 2 * len(CC) + 2 * 2 + 1


def pool_takes(layer, pair):
    return layer == 0 or pair % 2 == 1


class Batch:

    def __init__(self, i, off=0):
        self.i, self.off = i, off
        self.fixed = isinstance(i, int)

    def at(self, each, k):
        if each == 1:
            return self.i + (self.off + k)
        return self.i * each + (self.off * each + k)

    def index(self):
        return self.i + self.off

    def reached(self, eng, sem, each, k):
        if self.fixed and self.at(each, k) <= 0:
            return
        eng.wait_ge(sem, self.at(each, k))


AHEAD = ({"xh": 1, "xl": 1, "xt": 1, "q": 1, "s": 1, "m": 1, "v": 1, "res": 1, "t": 0, "a": 0, "x": 0, "o": 0},
         {"xh": 0, "xt": 0, "xl": -1, "q": -1, "s": -1, "m": -1, "v": -1, "g": -1, "vb": -1, "res": -1, "t": -1,
          "a": -2, "sem": -2, "fx": -2, "ks": -2, "at": -2, "pt": -2, "ip": -2, "x": -2, "o": -2})

ORDER = {
    "pe": """
        1a0@7 0t0@4 1a1@3 0t1@5 1a2@1 0t2@2 1a3@6 0t3@0 1a4@4 1q0@5 0t4@2 1a5@6 1a6@3 1q1@4 0t5@5 1q2@7 0t6@0 1a7@1
        1s0@5 0t7@7 0t8@6 0t9@4 1s1@6 1s2@0 1s3@1 0q0@5 1s4@6 0q1@4 1s5@7 0q2@5 0a0@2 0a1@3 1s6@0 1s7@1 1s8@2 0x0@7
        0x1@3 0x2@4 1pt0@6 1s9@7 0o0@3 1ip0@6 1m0@1 1ip1@0 0o1@5 0o2@4 1t0@6 0s0@7 0s1@1 0s2@0 0s3@3 1x0@2 1t1@5
        1t2@4 0s4@7 0s5@6 1x1@0 0s6@2 1t3@1 1t4@3 1x2@7 1t5@5 0s7@4 1t6@0 0s8@6 1t7@1 1t8@2 0s9@3 1o0@4 1o1@5 1t9@0
        0m0@3 1o2@6""",
    "act": """
        1a0 0t0 1a1 0t1 1a2 0t2 1a3 1a4 0t3 1q0 0t4 1a5 1a6 1q1 0t5 1q2 1a7 0t6 0t7 0t8 1s0 0t9 0q0 1s1 1s2 0q1 0q2
        1s3 1s4 1fx0 1s5 0x0 0x1 0x2 1s6 1pt0 1s7 1s8 1m0 1s9 1t0 1x0 1t1 1x1 1t2 1t3 1x2 1t4 1t5 1t6 1t7 0m0 1t8
        1t9""",
    "dve": """
        1a0 1a1 1a2 1a3 1a4 1q0 1a5 1q1 1a6 1q2 1a7 1sem0 1sem1 1sem2 1s0 1sem3 1sem4 1sem5 1sem6 0xt0 1sem7 1s1
        1sem8 1sem9 1sem10 1s2 1sem11 0q0 1sem12 1s3 1sem13 1sem14 1s4 1sem15 1sem16 0q1 1sem17 1sem18 0q2 1sem19
        1s5 1sem20 0a0 1sem21 0a1 1sem22 1s6 1sem23 1sem24 0x0 0x1 0x2 1s7 1s8 1s9 0o0 1ip0 1ip1 1g0 0o1 0o2 1m0 0s0
        0s1 0s2 1x0 0s3 0s4 0s5 1t0 0s6 1x1 1t2 1x2 0s7 1xh0 0s8 0s9 1xt0 1o0 1t4 1o1 1t6 1o2 0m0 1t8""",
    "pool": """
        1xl0 0t0 0t1 0t2 1ks0 0t3 1res0 0t4 1res1 0xh0 0xl0 0t5 0t6 0t7 0t8 0t9 1res2 1at0 1v0 0v0 1vb0 1t1 0res0
        1t3 1t5 0res1 0res2 1t7 1t9""",
}


def steps_of(engine):
    out = []
    for word in ORDER[engine].split():
        word = word.split("@")[0]
        name = word[1:].rstrip("0123456789")
        out.append((int(word[0]), AHEAD[int(word[0])][name], name, int(word[1 + len(name):])))
    return out


FIRST_ALIKE = 3


class Ring:

    def __init__(self):
        banks = [int(word.split("@")[1]) for word in ORDER["pe"].split()]
        self.on = [[] for _ in range(RING)]
        self.of = {}
        for r, (l, off, name, n) in zip(banks, steps_of("pe")):
            self.of[l, f"{name}{n}"] = (r, len(self.on[r]), off)
            self.on[r].append((l, off, name, n))

    def bank(self, layer, use):
        return self.of[layer, use][0]

    def order(self, layer, use):
        r, k, off = self.of[layer, use]
        return k - off * len(self.on[r])

    def done(self, r, turn, k):
        def there(t, steps):
            return sum(0 <= t + off < B for _, off, _, _ in steps)
        return sum(there(t, self.on[r]) for t in range(-1, turn)) + there(turn, self.on[r][:k])

    def wait(self, eng, sems, b, layer, use, more):
        r, k, off = self.of[layer, use]
        shift = b.off - off
        if b.fixed:
            if 0 <= b.i + b.off and self.done(r, b.i + shift, k) + more > 0:
                eng.wait_ge(sems[r], self.done(r, b.i + shift, k) + more)
            return
        each = len(self.on[r])
        eng.wait_ge(sems[r], b.i * each + ((shift - FIRST_ALIKE) * each + self.done(r, FIRST_ALIKE, k) + more))


def inverse_root(eng, done, sq, y, t):
    done(eng.tensor_scalar(y.bitcast(I32), sq.bitcast(I32), 1, None, ALU.logical_shift_right))
    done(eng.tensor_scalar(y.bitcast(I32), y.bitcast(I32), -1.0, float(MAGIC), ALU.mult, ALU.add))
    for _ in range(NEWTON):
        done(eng.tensor_tensor(t, y, y, ALU.mult))
        done(eng.scalar_tensor_tensor(t, t, -0.5, sq, ALU.mult, ALU.mult))
        done(eng.scalar_tensor_tensor(y, t, 1.5, y, ALU.add, ALU.mult))


def keys_and_values(nc, psum, ctx, ctxip, wk, wv, wq, wo, wk_ip, wv_ip, k_dram, v_dram, g_dram, vip_dram, wqs, wos,
                    rnorm4):
    both = (0, 1)
    PAIRS = B // CB // 2
    with ExitStack() as stack:
        def sb(name, shape, dt=F32):
            return stack.enter_context(nc.sbuf_tensor(name, shape, dt))

        def sem(name):
            return stack.enter_context(nc.semaphore(name))

        raw = {}
        split = {}
        for name, columns in (("k0", TAIL), ("k1", TAIL), ("kt", P), ("ki", C), ("v0", C), ("v1", C)):
            raw[name] = sb(f"raw_{name}", [P, EC, columns])
            split[name] = sb(f"split_{name}", [P, 2, EC, columns], F16)
        for l in both:
            for name, t in ((f"q{l}", wqs[l]), (f"o{l}", wos[l])):
                raw[name] = sb(f"raw_{name}", [P, 3, C])
                split[name] = t
        order = ["k0", "k1", "kt", "ki", "v0", "v1", "q0", "o0", "q1", "o1"]
        loads = {name: 1 for name in order} | {"kt": 2, "q0": 3, "o0": 3, "q1": 3, "o1": 3}
        wvi = sb("wvi", [P, EC, C])
        ones = sb("ones", [P, P])
        one = sb("one", [P, EC])
        ctxip_sb = sb("ctxip_sb", [P, EC, B * IP])
        ipsq = sb("ipsq", [P, EC, B * IP])
        ipss = sb("ipss", [P, B * IP])
        ipy = sb("ipy", [P, B * IP])
        ipt = sb("ipt", [P, B * IP])
        vip = sb("vip", [P, 2, C])
        cx = sb("cx", [P, 2, EC, CT])
        ch = sb("ch", [P, 2, EC, CT], F16)
        cl = sb("cl", [P, 2, EC, CT], F16)
        kst = [sb(f"kst{l}", [P, 2, FULL, 2, CT], F16) for l in both]
        ktail = sb("ktail", [P, 2, 2, CT], F16)
        vst = [sb(f"vst{l}", [P, 2, len(VT), 2, C], F16) for l in both]
        gst = sb("gst", [P, 2, CB, 2, T], F16)

        s_raw = {name: sem(f"raw_{name}_loaded") for name in order}
        s_ip = sem("ip_loaded")
        s_one = sem("one_written")
        s_wh, s_wl = sem("weights_high"), sem("weights_low")
        s_ctx = [sem(f"context_loaded{slot}") for slot in (0, 1)]
        s_ch, s_cl = sem("context_high"), sem("context_low")
        s_filled, s_high, s_freed = sem("kv_filled"), sem("kv_high"), sem("kv_freed")
        s_stored = [sem(f"kv_stored{slot}") for slot in (0, 1)]
        s_ipsq, s_ipf, s_vip, s_chain = sem("ip_squares"), sem("ip_filled"), sem("vip_read"), sem("ip_chain")
        s_last = sem("vip_stored")

        def pairs(eng, chunk, image_tokens=lambda: None):
            for slot in (0, 1):
                chunk(Batch(0), slot)
            image_tokens()
            with eng.Fori(1, PAIRS) as i:
                for slot in (0, 1):
                    chunk(Batch(i), slot)

        block = stack.enter_context(nc.Block())

        @block.sync
        def _(sp):
            def load_weight(name, src):
                if name == "kt":
                    for l in both:
                        sp.dma_start(raw[name][:, :, l * HALF:(l + 1) * HALF],
                                     wk[l][:, TAIL:C].rearrange("(k p) n -> p k n", p=P)).then_inc(s_raw[name], 16)
                elif name[0] in "kv":
                    src = src[:, 0:raw[name].shape[2]]
                    sp.dma_start(raw[name][:], src.rearrange("(k p) n -> p k n", p=P)).then_inc(s_raw[name], 16)
                else:
                    sp.dma_start(raw[name][:, 0:2, :], src[0:256, :].rearrange("(k p) n -> p k n", p=P))\
                      .then_inc(s_raw[name], 16)
                    for half in (0, 1):
                        sp.dma_start(raw[name][half * HALF:(half + 1) * HALF, 2, :], src[256:320, :])\
                          .then_inc(s_raw[name], 16)

            def load_context(b, slot):
                src = ctx[:, bass.DynSlice(b.at(2 * CT, slot * CT), CT)].rearrange("(k p) n -> p k n", p=P)
                b.reached(sp, s_cl, 2, slot + 1 - 2)
                sp.dma_start(cx[:, slot, :, :], src).then_inc(s_ctx[slot], 16)

            def store(b, slot):
                batch = b.at(2 * CB, slot * CB)
                token = b.at(2 * CT, slot * CT)

                def results_of(*kinds):
                    last = max(u for u in range(KU) if KV_USES[u][0:2] in kinds)
                    b.reached(sp, s_freed, 2 * KU, slot * KU + last + 1)

                results_of(("kt", 0), ("ki", 1))
                for l in both:
                    for c, (c0, m) in reversed(list(enumerate(CC))):
                        dst = k_dram[l][:, c0:c0 + m, bass.DynSlice(token, CT)].rearrange("h c n -> c h n")
                        keys = kst[l][:, slot, c, :, :] if c < FULL else ktail[l * HALF:(l + 1) * HALF, slot, :, :]
                        sp.dma_start(dst, keys).then_inc(s_stored[slot], 16)
                results_of(("g", 1))
                dst = g_dram[bass.DynSlice(batch, CB), :, :].rearrange("b t n -> t b n")
                sp.dma_start(dst, gst[0:TXT[1], slot, :, :, :].rearrange("t b h n -> t b (h n)"))\
                  .then_inc(s_stored[slot], 16)
                full = len(VT) - 1
                for l in both:
                    results_of(("v", l))
                    dst = v_dram[l][bass.DynSlice(token, full * P), :].rearrange("(k p) n -> p k n", p=P)
                    sp.dma_start(dst, vst[l][:, slot, 0:full, :, :].rearrange("p k h n -> p k (h n)"))\
                      .then_inc(s_stored[slot], 16)
                    dst = v_dram[l][bass.DynSlice(token + full * P, VT[-1][1]), :]
                    sp.dma_start(dst, vst[l][0:VT[-1][1], slot, full, :, :].rearrange("p h n -> p (h n)"))\
                      .then_inc(s_stored[slot], 16)

            source = {"k0": wk[0], "k1": wk[1], "kt": None, "ki": wk_ip, "v0": wv[0], "v1": wv[1], "q0": wq[0],
                      "q1": wq[1], "o0": wo[0], "o1": wo[1]}
            load_weight("k0", source["k0"])
            load_context(Batch(0), 0)
            for name in order[1:6]:
                load_weight(name, source[name])
            load_context(Batch(0), 1)
            for name in order[6:]:
                load_weight(name, source[name])
            sp.dma_start(wvi[:], wv_ip.rearrange("(k p) n -> p k n", p=P)).then_inc(s_ip, 16)
            sp.dma_start(ctxip_sb[:], ctxip.rearrange("(k p) n -> p k n", p=P)).then_inc(s_ip, 16)
            for slot in (0, 1):
                load_context(Batch(1), slot)
            for slot in (0, 1):
                store(Batch(0), slot)
            sp.wait_ge(s_vip, 2)
            for k in range(2):
                sp.dma_start(vip_dram[k * P:(k + 1) * P, :], vip[:, k, :]).then_inc(s_last, 16)
            with sp.Fori(2, PAIRS) as i:
                for slot in (0, 1):
                    load_context(Batch(i), slot)
                for slot in (0, 1):
                    store(Batch(i, -1), slot)
            for slot in (0, 1):
                store(Batch(PAIRS - 1), slot)
            sp.wait_ge(s_last, 32)
            for slot in (0, 1):
                sp.wait_ge(s_stored[slot], 16 * KV_STORES * PAIRS)

        @block.tensor
        def _(pe):
            def three(out, parts):
                for n, (a, b) in enumerate(parts):
                    mm = pe.matmul(out, a, b, start=(n == 0), stop=(n == len(parts) - 1))
                return mm

            def products(wname, c0, m, rhs):
                w = split[wname]
                return [(w[:, hw, k, c0:c0 + m], rhs(hc, k)) for k in range(EC) for hw, hc in ((0, 0), (1, 0), (0, 1))]

            def chunk(b, slot):
                b.reached(pe, s_cl, 2, slot + 1)
                parts = (ch, cl)
                for u, (kind, l, c, half) in enumerate(KV_USES):
                    before = u - RING if u >= RING else max(v for v in range(KU) if v % RING == u) - KU
                    b.reached(pe, s_freed, 2 * KU, slot * KU + before + 1)
                    r = u % RING
                    if b.fixed and slot == 0 and kind != "g":
                        pe.wait_ge(s_wl, order.index(kind if len(kind) == 2 else f"{kind}{l}") + 1)
                    if kind in ("k", "kt"):
                        n = TXT[l] if kind == "k" else T

                        def tokens(h, k):
                            cols = parts[h][:, slot, k, half * HT:(half + 1) * HT]
                            return cols.rearrange("p (b t) -> p b t", t=T)[:, :, 0:n]
                        o = psum[:, r, 0:HT].rearrange("p (b t) -> p b t", t=T)
                        mm = three(o[:, :, 0:n], products(f"k{l}" if kind == "k" else kind, c * P, P, tokens))
                    elif kind == "ki":
                        def images(h, k):
                            return parts[h][:, slot, k, :].rearrange("p (b t) -> p b t", t=T)[:, :, TXT[1]:]
                        for c in range(len(CC)):
                            o = psum[:, r, c * CB * IP:(c + 1) * CB * IP].rearrange("p (b t) -> p b t", t=IP)
                            mm = three(o, products(kind, min(c * P, C - P), P, images))
                    elif kind == "v":
                        k0, m = VT[c]
                        w = split[f"v{l}"]
                        mm = three(psum[0:m, r, 0:C],
                                   [(parts[hc][:, slot, k, k0:k0 + m], w[:, hw, k, :])
                                    for k in range(EC) for hc, hw in ((0, 0), (0, 1), (1, 0))])
                    else:
                        for j in range(HB):
                            t0 = half * HT + j * T
                            mm = three(psum[0:TXT[1], r, j * T:(j + 1) * T],
                                       [(parts[h1][:, slot, k, t0:t0 + TXT[1]], parts[h2][:, slot, k, t0:t0 + T])
                                        for k in range(EC) for h1, h2 in ((0, 0), (0, 1), (1, 0))])
                    mm.then_inc(s_filled, 1)

            def image_tokens():
                pe.wait_ge(s_freed, KU + max(u for u in range(KU) if u % RING < 3) + 1)
                pe.wait_ge(s_ipsq, 2)
                pe.wait_ge(s_ip, 32)
                for j in range(2):
                    for k in range(EC):
                        mm = pe.matmul(psum[:, j, 0:C], ctxip_sb[:, k, j * P:(j + 1) * P], wvi[:, k, :],
                                       start=(k == 0), stop=(k == EC - 1))
                    mm.then_inc(s_ipf, 1)
                for k in range(EC):
                    mm = pe.matmul(psum[:, 2, 0:B * IP], ones[:], ipsq[:, k, :], start=(k == 0), stop=(k == EC - 1))
                mm.then_inc(s_ipf, 1)
                pe.wait_ge(s_vip, 2)
                pe.wait_ge(s_chain, 1)

            pairs(pe, chunk, image_tokens)

        def results(u, slot):
            kind, l, c, half = KV_USES[u]
            r = u % RING

            def by_batch(ap, t):
                return ap.rearrange("p (b t) -> p b t", t=t)
            if kind == "v":
                m = VT[c][1]
                return [(psum[0:m, r, 0:C], [vst[l][0:m, slot, c, h, :] for h in both], 1 / WS)]
            if kind == "g":
                return [(by_batch(psum[0:TXT[1], r, 0:HT], T),
                         [gst[0:TXT[1], slot, half * HB:(half + 1) * HB, h, :] for h in both], GS)]
            tokens = slice(half * HT, (half + 1) * HT)
            if kind == "k":
                return [(by_batch(psum[:, r, 0:HT], T)[:, :, 0:TXT[l]],
                         [by_batch(kst[l][:, slot, c, h, tokens], T)[:, :, 0:TXT[l]] for h in both], 1 / WS)]
            if kind == "kt":
                rows = [slice(layer * HALF, (layer + 1) * HALF) for layer in both]
                return [(by_batch(psum[rows[layer], r, 0:HT], T)[:, :, 0:TXT[layer]],
                         [by_batch(ktail[rows[layer], slot, h, tokens], T)[:, :, 0:TXT[layer]] for h in both],
                         1 / WS) for layer in both]
            out = []
            for c in range(len(CC)):
                rows = slice(0, P) if c < FULL else slice(HALF, P)
                keys = [kst[l][:, slot, c, h, :] if c < FULL else ktail[rows, slot, h, :] for h in both]
                out.append((by_batch(psum[rows, r, c * CB * IP:(c + 1) * CB * IP], IP),
                            [by_batch(k, T)[:, :, TXT[1]:] for k in keys], 1 / WS))
            return out

        @block.scalar
        def _(act):
            for n, name in enumerate(order):
                act.wait_ge(s_raw[name], 16 * loads[name])
                act.activation(split[name][:, 0, :, :], raw[name][:], ACT.Copy, scale=WS).then_inc(s_wh, 1)
                if n == 0:
                    act.wait_ge(s_ctx[0], 16)
                    act.activation(ch[:, 0, :, :], cx[:, 0, :, :], ACT.Copy).then_inc(s_ch, 1)

            def chunk(b, slot):
                b.reached(act, s_stored[slot], 16 * KV_STORES, 0)
                for u in range(KU):
                    b.reached(act, s_filled, 2 * KU, slot * KU + u + 1)
                    for source, (high, _), scale in results(u, slot):
                        ins = act.activation(high, source, ACT.Copy, scale=scale)
                    ins.then_inc(s_high, 1)

            def image_tokens():
                for j in range(2):
                    act.wait_ge(s_ipf, j + 1)
                    act.activation(vip[:, j, :], psum[:, j, 0:C], ACT.Copy).then_inc(s_vip, 1)

            pairs(act, chunk, image_tokens)

        @block.vector
        def _(dve):
            for n, name in enumerate(order):
                dve.wait_ge(s_wh, n + 1)
                t = split[name]
                dve.scalar_tensor_tensor(t[:, 1, :, :], raw[name][:], WS, t[:, 0, :, :], ALU.mult, ALU.subtract)\
                   .then_inc(s_wl, 1)
                if n == 0:
                    dve.wait_ge(s_ch, 1)
                    dve.tensor_tensor(cl[:, 0, :, :], cx[:, 0, :, :], ch[:, 0, :, :], ALU.subtract).then_inc(s_cl, 1)
            dve.memset(ones[:], 1.0).then_inc(s_ipsq, 1)
            dve.wait_ge(s_ip, 32)
            dve.tensor_tensor(ipsq[:], ctxip_sb[:], ctxip_sb[:], ALU.mult).then_inc(s_ipsq, 1)

            def chunk(b, slot):
                for u in range(KU):
                    b.reached(dve, s_high, 2 * KU, slot * KU + u + 1)
                    for source, (high, low), scale in results(u, slot):
                        ins = dve.scalar_tensor_tensor(low, source, scale, high, ALU.mult, ALU.subtract)
                    ins.then_inc(s_freed, 1)

            count = [0]

            def done(ins):
                count[0] += 1
                ins.then_inc(s_chain, 1)
                dve.wait_ge(s_chain, count[0])

            def image_tokens():
                dve.wait_ge(s_ipf, 3)
                done(dve.tensor_scalar(ipss[:], psum[:, 2, 0:B * IP], EPS * EPS, None, ALU.max))
                inverse_root(dve, done, ipss[:], ipy[:], ipt[:])
                done(dve.tensor_scalar(rnorm4[:].rearrange("p b n -> p (b n)"), ipy[:], 4.0, None, ALU.mult))

            pairs(dve, chunk, image_tokens)

        @block.gpsimd
        def _(pool):
            pool.memset(one[:], 1.0).then_inc(s_one, 1)
            pool.wait_ge(s_one, 1)

            def chunk(b, slot):
                if b.fixed and slot == 0:
                    pool.wait_ge(s_cl, 1)
                    return
                b.reached(pool, s_ctx[slot], 16, 16)
                b.reached(pool, s_filled, 2 * KU, (slot - 1) * KU)
                pool.tensor_tensor(ch[:, slot, :, :], cx[:, slot, :, :],
                                   one[:].unsqueeze(2).to_broadcast([P, EC, CT]), ALU.mult).then_inc(s_ch, 1)
                b.reached(pool, s_ch, 2, slot + 1)
                pool.tensor_tensor(cl[:, slot, :, :], cx[:, slot, :, :], ch[:, slot, :, :], ALU.subtract)\
                    .then_inc(s_cl, 1)

            pairs(pool, chunk)


def attention(nc, psum, x, mask, bias, ident_d, ident16_d, ipmask_d, ind_d, k_dram, v_dram, g_dram, vip_dram, wqs, wos,
              rnorm4, out):
    both = (0, 1)
    with ExitStack() as stack:
        def sb(name, shape, dt=F32):
            return stack.enter_context(nc.sbuf_tensor(name, shape, dt))

        def sem(name):
            return stack.enter_context(nc.semaphore(name))

        ring = Ring()

        ident = sb("ident", [P, P])
        one = sb("one16", [P, H])
        ident16 = sb("ident16", [P, P], F16)
        ipmask = sb("ipmask", [H * IP, H])
        mask_sb = sb("mask_sb", [P, SC])
        bias_sb = [sb(f"bias{l}", [P, 3]) for l in both]
        xin = [sb(f"x{l}", [P, 3, S]) for l in both]
        xs = [sb(f"xs{l}", [P, 2, 3, S], F16) for l in both]
        res = [sb(f"res{l}", [P, 3, S]) for l in both]
        res_next = sb("res_next", [P, 3, S])
        kb = [sb(f"kb{l}", [P, GH, 2, G, T], F16) for l in both]
        vst = [sb(f"values{l}", [T, 2, C], F16) for l in both]
        gst = sb("gram", [T, 2, T], F16)
        vh = [sb(f"vh{l}", [P, H, VW[l]], F16) for l in both]
        vl = [sb(f"vl{l}", [P, H, VW[l]], F16) for l in both]
        qs = [sb(f"qs{l}", [P, G, S], F16) for l in both]
        qm = [sb(f"qm{l}", [P, G, S], F16) for l in both]
        nm = sb("nm", [P, SC, H])
        mneg = [sb(f"mneg{l}", [P, SC, P], F16) for l in both]
        ef = [sb(f"ef{l}", [P, EF, PAIR * S]) for l in both]
        eh = [sb(f"eh{l}", [P, H, S], F16) for l in both]
        el = [sb(f"el{l}", [P, H, S], F16) for l in both]
        est = sb("est", [P, SC, H, TXT[1]])
        rd = [sb(f"rd{l}", [P, SC, H]) for l in both]
        at = [sb(f"at{l}", [P, SC, 3 * P]) for l in both]
        att = [sb(f"att{l}", [P, 2, 3, S], F16) for l in both]
        sip = sb("sip", [P, SC, H, IP])
        sip2 = sb("sip2", [P, SC, H, IP])
        ust = sb("ust", [P, SC, H, D + 1])
        ast = sb("ast", [P, SC, H, IP])
        pe_ = sb("pe_", [P, 2, QH, TXT[1]])
        n2 = sb("n2", [P, SC, H])
        ny = sb("ny", [P, SC, H])
        nt = sb("nt", [P, SC, H])
        lim = sb("lim", [P, SC, H])
        fu = sb("fu", [P, SC, H, IP])
        fm = sb("fm", [P, SC, H])
        pip = sb("pip", [P, SC, H, IP])
        pt = sb("pt", [P, S])
        viprow = sb("viprow", [H * IP, C])
        vbip = sb("vbip", [P, C])
        outt = sb("outt", [P, 3, S])

        def pair(name):
            return [sem(f"{name}{l}") for l in both]
        filled = [sem(f"filled_{r}") for r in range(RING)]
        freed = [sem(f"freed_{r}") for r in range(RING)]
        s_w = sem("constants_loaded")
        s_ind = pair("head_picks_loaded")
        s_zero_dve, s_zero_pool, s_zero_act = sem("cleared_by_dve"), sem("cleared_by_pool"), sem("cleared_by_act")
        s_x = sem("x_loaded")
        s_kb, s_vst, s_gst = pair("key_blocks_loaded"), pair("values_loaded"), sem("gram_loaded")
        s_viprow = sem("vip_rows_loaded")
        s_store = sem("out_stored")
        s_moved = sem("residual1_moved")
        s_res = pair("residual_")
        s_xh, s_xl, s_xt = pair("x_high"), pair("x_low"), pair("x_tail_low")
        s_v, s_gr = pair("value_table"), sem("gram_spread")
        s_qh, s_qm = pair("q_high"), pair("q_copied")
        s_mr, s_mx = sem("maxima_rounded"), sem("maxima")
        s_ms = pair("maxima_spread")
        s_el = pair("exp_low_dve"), pair("exp_low_pool")
        s_rd = pair("den_inverse")
        s_sip, s_ast, s_n2 = sem("ip_scores"), sem("ip_products"), sem("square_norms")
        s_semd, s_fe, s_vb = sem("ip_softmax_steps"), sem("ip_exp"), sem("vip_blocks")
        s_pip = sem("ip_probabilities")
        s_at0 = sem("text_attended")
        s_sip2 = sem("ip_scores_kept")
        s_ath = pair("attended_high")
        SEMD = 14 + 3 * NEWTON
        KB_LOADS = 2 * GH

        def bank(l, use):
            return psum[:, ring.bank(l, use), :]

        def previous(b):
            return Batch(b.i, b.off - 1)

        def wait_fill(eng, l, b, use, before=False):
            ring.wait(eng, filled, previous(b) if before else b, l, use, 1)

        def wait_free(eng, l, b, use, reads=()):
            latest = {ring.bank(l, use): (ring.order(l, use), use, 0)}
            for other in reads:
                r, k = ring.bank(l, other), ring.order(l, other) + 1
                if r not in latest or latest[r][0] < k:
                    latest[r] = (k, other, 1)
            for _, other, more in latest.values():
                ring.wait(eng, freed, b, l, other, more)

        def fill_sem(l, use):
            return filled[ring.bank(l, use)]

        def wait_read(eng, l, b, use, before=False):
            ring.wait(eng, freed, previous(b) if before else b, l, use, 1)

        def free_sem(l, use):
            return freed[ring.bank(l, use)]

        def low_done(l, p):
            def mine(upto, on_pool):
                return sum(pool_takes(l, q) == on_pool for q in range(upto))
            on_pool = pool_takes(l, p)
            return s_el[on_pool][l], mine(NP, on_pool), mine(p + 1, on_pool)

        def low_parts(eng, l, b, p):
            n = TXT[l]
            wait_read(eng, l, b, f"t{p}")
            eng.tensor_tensor(el[l][0:n, p * PAIR:(p + 1) * PAIR, :],
                              ef[l][0:n, p % EF, :].rearrange("t (h s) -> t h s", s=S),
                              eh[l][0:n, p * PAIR:(p + 1) * PAIR, :], ALU.subtract).then_inc(low_done(l, p)[0], 1)

        def turns(eng, turn, before={}, shift=0):
            for i in range(-1, FIRST_ALIKE):
                before.get(i, lambda: None)()
                turn(i)
            assert (B - 1 - FIRST_ALIKE) % 2 == 0
            with eng.Fori(FIRST_ALIKE + shift, B - 2 + shift, 2) as i:
                turn(i, -shift)
                turn(i, 1 - shift)
            for i in range(B - 1, B + 2):
                turn(i)

        def program(eng, order, steps, before={}):
            def turn(i, later=0):
                for layer, off, name, n in order:
                    if not isinstance(i, int) or 0 <= i + off < B:
                        steps[name](layer, Batch(i, off + later), n)

            def all_clear():
                eng.wait_ge(s_zero_dve, DVE_CLEARS)
                eng.wait_ge(s_zero_pool, POOL_CLEARS)
            turns(eng, turn, {1: all_clear} | before)

        dve_clears = ([kb[0], mneg[0], vh[0], vl[0]], [kb[1], mneg[1], vh[1], vl[1]])
        pool_clears = ([xin[0], at[0], xin[1]], [eh[1], el[1], at[1], pt, vbip])
        act_clears = [eh[0], el[0]]
        DVE_FIRST, POOL_FIRST = len(dve_clears[0]) + 1, len(pool_clears[0]) + 1
        DVE_CLEARS = DVE_FIRST + len(dve_clears[1]) + 1
        POOL_CLEARS = POOL_FIRST + len(pool_clears[1])
        WEIGHTS = 10
        block = stack.enter_context(nc.Block())

        @block.sync
        def _(sp):
            def load_constants():
                n = 0
                for t, d in [(ident16, ident16_d), (ident, ident_d), (ipmask, ipmask_d), (mask_sb, mask)]:
                    sp.dma_start(t[:], d).then_inc(s_w, 16)
                    n += 1
                for l in both:
                    for c, (c0, m) in enumerate(CC):
                        sp.dma_start(bias_sb[l][0:m, c:c + 1], bias[l][c0:c0 + m, :]).then_inc(s_w, 16)
                        n += 1
                assert n == WEIGHTS

            def load_x(b):
                b.reached(sp, s_xl[0], 1, 0)
                b.reached(sp, s_xt[0], 1, 0)
                b.reached(sp, s_res[0], 1, 0)
                src = x[bass.DynSlice(b.index(), 1), :, :].rearrange("a c s -> (a c) s")
                sp.dma_start(xin[0][:, 0:2, :], src[0:256, :].rearrange("(k p) s -> p k s", p=P)).then_inc(s_x, 16)
                sp.dma_start(xin[0][0:64, 2, :], src[256:320, :]).then_inc(s_x, 16)

            def load_keys(l, b):
                src = k_dram[l].rearrange("h (g j d) n -> j d (h g) n", g=G, j=GH)
                tokens = bass.DynSlice(b.index() * T, T)
                wait_fill(sp, l, b, f"t{NP - 1}", before=True)
                for j in reversed(range(GH)):
                    for r, parts in ((0, 2), (1, 1)):
                        p0 = r * HALF + j * D
                        dst = kb[l][p0:p0 + D, j, 0:parts, :, :].rearrange("p h g t -> p (h g) t")
                        sp.dma_start(dst, src[j, :, 0:parts * G, tokens]).then_inc(s_kb[l], 16)

            def load_values(l, b):
                src = v_dram[l][bass.DynSlice(b.index() * T, T), :]
                b.reached(sp, s_v[l], 2, 0)
                sp.dma_start(vst[l][:].rearrange("t h n -> t (h n)"), src).then_inc(s_vst[l], 16)

            def load_gram(b):
                b.reached(sp, s_gr, 2, 0)
                src = g_dram[bass.DynSlice(b.index(), 1), :, :].rearrange("b t n -> (b t) n")
                sp.dma_start(gst[0:TXT[1], :, :].rearrange("t h n -> t (h n)"), src).then_inc(s_gst, 16)

            def load_vip(b):
                b.reached(sp, s_vb, 1, 0)
                src = vip_dram[bass.DynSlice(b.index() * IP, IP), :]
                sp.dma_start(viprow[:], src.unsqueeze(0).to_broadcast([H, IP, C])).then_inc(s_viprow, 16)

            def move_residual(b):
                b.reached(sp, s_res[1], 1, 1)
                sp.dma_start(res[1][:, 0:2, :], res_next[:, 0:2, :]).then_inc(s_moved, 16)
                sp.dma_start(res[1][0:64, 2, :], res_next[0:64, 2, :]).then_inc(s_moved, 16)

            def store(b):
                wait_read(sp, 1, b, "o2")
                dst = out[bass.DynSlice(b.index(), 1), :, :].rearrange("a c s -> (a c) s")
                sp.dma_start(dst[0:256, :].rearrange("(k p) s -> p k s", p=P), outt[:, 0:2, :]).then_inc(s_store, 16)
                sp.dma_start(dst[256:320, :], outt[0:64, 2, :]).then_inc(s_store, 16)

            def load_picks(l, clears):
                sp.wait_ge(s_zero_dve, clears)
                sp.dma_start(kb[l][HALF:P, :, 1, :, :], ind_d.rearrange("p (j g t) -> p j g t", j=GH, g=G))\
                  .then_inc(s_ind[l], 16)

            def turn(i, later=0):
                def there(off):
                    return not isinstance(i, int) or 0 <= i + off < B
                if there(-1):
                    if isinstance(i, int) and i == 1:
                        load_picks(1, DVE_CLEARS)
                    load_keys(1, Batch(i, later - 1))
                if there(1):
                    load_x(Batch(i, later + 1))
                    if isinstance(i, int) and i == -1:
                        load_constants()
                    load_values(0, Batch(i, later + 1))
                if there(-1):
                    load_values(1, Batch(i, later - 1))
                    load_gram(Batch(i, later - 1))
                    load_vip(Batch(i, later - 1))
                if there(1):
                    if isinstance(i, int) and i == -1:
                        load_picks(0, DVE_FIRST)
                    load_keys(0, Batch(i, later + 1))
                if there(-2):
                    store(Batch(i, later - 2))
                if there(-1):
                    move_residual(Batch(i, later - 1))
            sp.wait_ge(s_zero_pool, 1)
            turns(sp, turn, shift=3)
            sp.wait_ge(s_store, 32 * B)

        @block.tensor
        def _(pe):
            pe.wait_ge(s_w, 16 * WEIGHTS)

            def project_split(o, w, c0, m, xparts):
                parts = [(w[:, hw, k, c0:c0 + m], xparts[:, hx, k, :])
                         for k in (0, 1) for hw, hx in ((0, 0), (1, 0), (0, 1))]
                parts += [(w[:, 0, 2, c0:c0 + m], xparts[:, 0, 2, :]),
                          (w[0:HALF, 1, 2, c0:c0 + m], xparts[0:HALF, 0, 2, :])]
                for n, (a, b) in enumerate(parts):
                    mm = pe.matmul(o, a, b, start=(n == 0), stop=(n == len(parts) - 1))
                return mm

            def query(l, b, c):
                c0, m = CC[c]
                wait_free(pe, l, b, f"q{c}")
                if c == 0:
                    b.reached(pe, s_xl[l], 1, 1)
                    b.reached(pe, s_xt[l], 1, 1)
                project_split(bank(l, f"q{c}")[0:m, 0:S], wqs[l], c0, m, xs[l]).then_inc(fill_sem(l, f"q{c}"), 1)

            def scores(l, b, n):
                s, g = divmod(n, G)
                use = f"s{n}"
                wait_free(pe, l, b, use, [f"q{g // 2}"] if s == 0 else [])
                if n == 0:
                    if l == 0 and b.fixed:
                        pe.wait_ge(s_zero_dve, DVE_FIRST)
                    if b.fixed:
                        pe.wait_ge(s_ind[l], 16)
                    b.reached(pe, s_kb[l], 16 * KB_LOADS, 16 * KB_LOADS)
                o = bank(l, use)[:, 0:GH * T].rearrange("p (h t) -> p h t", t=T)
                q = qs[l][:, g, s * P:(s + 1) * P]
                mm = pe.matmul(o, q, kb[l][:, :, 0, g, :], start=True, stop=(l == 0))
                if l:
                    mm = pe.matmul(o, q[0:HALF, :], kb[l][0:HALF, :, 1, g, :], start=False, stop=True)
                mm.then_inc(fill_sem(l, use), 1)

            def turn_max(l, b, n):
                wait_free(pe, l, b, "m0", [] if l else [f"s{k}" for k in range(SC * G)])
                if l:
                    b.reached(pe, s_mr, SC * G, SC * G)
                o = bank(l, "m0").bitcast(F16)
                for s in range(SC):
                    mm = pe.transpose(o[:, s * P:(s + 1) * P], mneg[l][:, s, :], ident16[:])
                mm.then_inc(fill_sem(l, "m0"), 1)

            def turned_scores(l, b, p):
                use = f"t{p}"
                wait_free(pe, l, b, use, ["m0"] if p == 0 else [])
                if p == 0:
                    b.reached(pe, s_qm[l], 1, 1)
                if p == GH // PAIR:
                    b.reached(pe, s_ms[l], 1, 1)
                for j in range(PAIR):
                    g, hj = divmod(p * PAIR + j, GH)
                    o = bank(l, use)[0:TXT[l], j * S:(j + 1) * S]
                    pe.matmul(o, kb[l][:, hj, 0, g, 0:TXT[l]], qs[l][:, g, :], start=True, stop=False)
                    mm = pe.matmul(o, kb[l][:, hj, 1, g, 0:TXT[l]], qm[l][:, g, :], start=False, stop=True)
                mm.then_inc(fill_sem(l, use), 1)

            def attend(l, b, n):
                use = f"a{n}"
                s, q = divmod(n, NQ) if l else (n, 0)
                heads = range(q * QH, (q + 1) * QH) if l else range(H)
                first, last = heads[0] // PAIR, heads[-1] // PAIR
                wait_free(pe, l, b, use, [f"t{p}" for p in range(first, last + 1)] if s == 0 else [])
                if s == 0:
                    for on_pool in {pool_takes(l, p) for p in range(NP)}:
                        p = max(p for p in range(last + 1) if pool_takes(l, p) == on_pool)
                        b.reached(pe, *low_done(l, p))
                if n == 0:
                    if b.fixed:
                        pe.wait_ge(s_zero_act, len(act_clears))
                    b.reached(pe, s_v[l], 2, 2)
                    if l:
                        b.reached(pe, s_gr, 2, 2)
                w = VW[l]
                for k, h in enumerate(heads):
                    o = bank(l, use)[:, k * w:(k + 1) * w]
                    e_h, e_l = eh[l][:, h, s * P:(s + 1) * P], el[l][:, h, s * P:(s + 1) * P]
                    pe.matmul(o, e_h, vh[l][:, h, :], start=True, stop=False)
                    pe.matmul(o, e_h, vl[l][:, h, :], start=False, stop=False)
                    mm = pe.matmul(o, e_l, vh[l][:, h, :], start=False, stop=True)
                mm.then_inc(fill_sem(l, use), 1)

            def turn_probs(l, b, n):
                wait_free(pe, l, b, "pt0")
                b.reached(pe, s_pip, 1, 1)
                for s in range(SC):
                    mm = pe.transpose(bank(l, "pt0")[0:H * IP, s * P:(s + 1) * P],
                                      pip[:, s, :, :].rearrange("p h n -> p (h n)"), ident[:])
                mm.then_inc(fill_sem(l, "pt0"), 1)

            def attend_ip(l, b, s):
                use = f"ip{s}"
                wait_free(pe, l, b, use, ["pt0"] if s == 0 else [])
                if s == 0:
                    b.reached(pe, s_vb, 1, 1)
                pe.matmul(bank(l, use)[:, 0:C], pt[:, s * P:(s + 1) * P], vbip[:],
                          start=True, stop=True).then_inc(fill_sem(l, use), 1)

            def turn_attended(l, b, c):
                wait_free(pe, l, b, f"x{c}", [f"{'ip' if l else 'a'}{s}" for s in range(SC)] if c == 0 else [])
                for s in range(SC):
                    mm = pe.transpose(bank(l, f"x{c}")[:, s * P:(s + 1) * P], at[l][:, s, c * P:(c + 1) * P], ident[:])
                mm.then_inc(fill_sem(l, f"x{c}"), 1)

            def project(l, b, c):
                c0, m = CC[c]
                wait_free(pe, l, b, f"o{c}", [f"x{k}" for k in range(3)] if c == 0 else [])
                project_split(bank(l, f"o{c}")[0:m, 0:S], wos[l], c0, m, att[l]).then_inc(fill_sem(l, f"o{c}"), 1)

            program(pe, steps_of("pe"), {"q": query, "s": scores, "m": turn_max, "t": turned_scores, "a": attend,
                                         "pt": turn_probs, "ip": attend_ip, "x": turn_attended, "o": project})

        @block.scalar
        def _(act):
            act.wait_ge(s_zero_pool, POOL_FIRST)
            for t in act_clears:
                zeros = at[0][:, 0, C:C + 1].unsqueeze(2).to_broadcast([P, H, S])
                act.activation(t[:], zeros, ACT.Copy).then_inc(s_zero_act, 1)

            def query(l, b, c):
                wait_fill(act, l, b, f"q{c}")
                if c == 0:
                    wait_fill(act, l, b, f"t{NP - 1}", before=True)
                for j in range(CC[c][1] // HALF):
                    act.activation(qs[l][0:HALF, 2 * c + j, :], bank(l, f"q{c}")[j * HALF:(j + 1) * HALF, 0:S],
                                   ACT.Copy, scale=SM / WS).then_inc(s_qh[l], 1)

            def scores(l, b, n):
                s, g = divmod(n, G)
                b.reached(act, s_mx, SC * G, n + 1)
                if n == 0:
                    wait_read(act, 1, b, f"a{AV[1] - 1}", before=True)
                    b.reached(act, s_sip2, 1, 0)
                o = bank(l, f"s{n}")[:, 0:GH * T].rearrange("p (h t) -> p h t", t=T)
                act.activation(sip[:, s, g * GH:(g + 1) * GH, :], o[:, :, TXT[1]:T], ACT.Copy).then_inc(s_sip, 1)
                for j in range(GH):
                    h = g * GH + j
                    ins = act.activation(est[:, s, h, :], o[:, j, 0:TXT[1]], ACT.Exp, bias=nm[:, s, h:h + 1])
                ins.then_inc(free_sem(l, f"s{n}"), 1)

            def turn_max(l, b, n):
                wait_fill(act, l, b, "m0")
                wait_fill(act, l, b, f"t{NP - 1}", before=True)
                act.activation(qm[l][HALF:P, 0, :], bank(l, "m0").bitcast(F16)[HALF:P, 0:S], ACT.Copy)\
                   .then_inc(free_sem(l, "m0"), 1)

            def turned_scores(l, b, p):
                use = f"t{p}"
                wait_fill(act, l, b, use)
                low, each, count = low_done(l, (p - EF) % NP)
                b.reached(act, low, each, count if p >= EF else count - each)
                n = TXT[l]
                act.activation(ef[l][0:n, p % EF, :], bank(l, use)[0:n, :], ACT.Exp)
                if p == 0:
                    wait_fill(act, l, b, f"a{AV[l] - 1}", before=True)
                act.activation(eh[l][0:n, p * PAIR:(p + 1) * PAIR, :],
                               bank(l, use)[0:n, :].rearrange("t (h s) -> t h s", s=S), ACT.Exp)\
                   .then_inc(free_sem(l, use), 1)

            def attend(l, b, n):
                s, q = divmod(n, NQ)
                wait_fill(act, l, b, f"a{n}")
                if n == 0:
                    b.reached(act, s_at0, 1, 0)
                o = bank(l, f"a{n}")[:, 0:QH * VW[1]].rearrange("p (h w) -> p h w", w=VW[1])
                act.activation(ust[:, s, q * QH:(q + 1) * QH, :], o[:, :, 0:D + 1], ACT.Copy)
                act.activation(ast[:, s, q * QH:(q + 1) * QH, :], o[:, :, D + 1 + TXT[1]:], ACT.Copy).then_inc(s_ast, 1)

            def fused_exp(l, b, n):
                b.reached(act, s_semd, SEMD, SEMD - 3)
                act.activation(fu[:], fu[:], ACT.Exp).then_inc(s_fe, 1)

            def turn_probs(l, b, n):
                wait_fill(act, l, b, "pt0")
                act.activation(pt[0:H * IP, :], bank(l, "pt0")[0:H * IP, 0:S], ACT.Copy).then_inc(free_sem(l, "pt0"), 1)

            def turn_attended(l, b, c):
                m = CC[c][1]
                wait_fill(act, l, b, f"x{c}")
                act.activation(att[l][0:m, 0, c, :], bank(l, f"x{c}")[0:m, 0:S], ACT.Copy).then_inc(s_ath[l], 1)

            program(act, steps_of("act"), {"q": query, "s": scores, "m": turn_max, "t": turned_scores, "a": attend,
                                           "fx": fused_exp, "pt": turn_probs, "x": turn_attended})

        @block.vector
        def _(dve):
            def clear(l):
                for t in dve_clears[l]:
                    dve.memset(t[:], 0.0).then_inc(s_zero_dve, 1)
                dve.wait_ge(s_zero_dve, (0, DVE_FIRST)[l] + len(dve_clears[l]))
                dve.memset(vh[l][0:TXT[l], :, D:D + 1], 1.0).then_inc(s_zero_dve, 1)

            clear(0)
            dve.wait_ge(s_w, 16 * WEIGHTS)
            dve.wait_ge(s_zero_dve, DVE_FIRST)
            dve.wait_ge(s_zero_pool, POOL_FIRST)

            def high_input(l, b, n):
                for c in range(3):
                    wait_read(dve, 0, b, f"o{c}")
                wait_fill(dve, l, b, "q2", before=True)
                dve.tensor_copy(xs[l][:, 0, :, :], xin[l][:]).then_inc(s_xh[l], 1)

            def low_tail(l, b, n):
                b.reached(dve, s_xh[l], 1, 1)
                dve.tensor_tensor(xs[l][HALF:P, 0, 2, :], xin[l][0:HALF, 2, :], xs[l][0:HALF, 0, 2, :], ALU.subtract)\
                   .then_inc(s_xt[l], 1)

            def gram(l, b, n):
                b.reached(dve, s_gst, 16, 16)
                wait_fill(dve, l, b, f"a{AV[l] - 1}", before=True)
                for h, t in enumerate((vh[1], vl[1])):
                    dve.tensor_copy(t[0:TXT[1], :, D + 1:],
                                    gst[0:TXT[1], h, :].unsqueeze(1).to_broadcast([TXT[1], H, T])).then_inc(s_gr, 1)

            def query(l, b, c):
                groups = CC[c][1] // HALF
                for j in range(groups):
                    g = 2 * c + j
                    b.reached(dve, s_qh[l], G, g + 1)
                    ins = dve.scalar_tensor_tensor(qs[l][HALF:P, g, :], bank(l, f"q{c}")[j * HALF:(j + 1) * HALF, 0:S],
                                                   SM / WS, qs[l][0:HALF, g, :], ALU.mult, ALU.subtract)
                ins.then_inc(free_sem(l, f"q{c}"), 1)
                if c == 2:
                    wait_fill(dve, l, b, f"t{NP - 1}", before=True)
                    dve.tensor_copy(qm[l][0:HALF, :, :], qs[l][0:HALF, :, :]).then_inc(s_qm[l], 1)

            def scores(l, b, n):
                s, g = divmod(n, G)
                wait_fill(dve, l, b, f"s{n}")
                if n == 0:
                    wait_fill(dve, l, b, "m0", before=True)
                o = bank(l, f"s{n}")[:, 0:GH * T].rearrange("p (h t) -> p h t", t=T)[:, :, 0:TXT[l]]
                m = mneg[l][:, s, HALF + g * GH:HALF + (g + 1) * GH]
                dve.tensor_reduce(m, o, AX_X, ALU.max, negate=True).then_inc(s_mr if l else free_sem(l, f"s{n}"), 1)
                if l:
                    if n == 0:
                        wait_read(dve, l, b, f"s{SC * G - 1}", before=True)
                    b.reached(dve, s_mr, SC * G, n + 1)
                    dve.tensor_copy(nm[:, s, g * GH:(g + 1) * GH], m).then_inc(s_mx, 1)

            def turn_max(l, b, n):
                wait_read(dve, l, b, "m0")
                dve.tensor_copy(qm[l][HALF:P, 1:, :], qm[l][HALF:P, 0:1, :].to_broadcast([HALF, G - 1, S]))\
                   .then_inc(s_ms[l], 1)

            def turned_scores(l, b, p):
                low_parts(dve, l, b, p)

            def attend(l, b, n):
                if l == 0:
                    wait_fill(dve, l, b, f"a{n}")
                    o = bank(l, f"a{n}")[:, 0:H * VW[0]].rearrange("p (h w) -> p h w", w=VW[0])
                    wait_read(dve, l, b, f"a{n}", before=True)
                    dve.reciprocal(rd[0][:, n, :], o[:, :, D]).then_inc(s_rd[0], 1)
                    b.reached(dve, s_rd[0], SC, n + 1)
                    wait_fill(dve, l, b, "x2", before=True)
                    dve.tensor_tensor(at[0][:, n, 0:C].rearrange("p (h d) -> p h d", d=D), o[:, :, 0:D],
                                      rd[0][:, n, :].unsqueeze(2).to_broadcast([P, H, D]), ALU.mult)\
                       .then_inc(free_sem(l, f"a{n}"), 1)
                    return
                s, q = divmod(n, NQ)
                b.reached(dve, s_ast, SC * NQ, n + 1)
                b.reached(dve, s_n2, SC * NQ, n - 1)
                o = bank(l, f"a{n}")[:, 0:QH * VW[1]].rearrange("p (h w) -> p h w", w=VW[1])
                dve.tensor_tensor(pe_[:, n % 2, :, :], o[:, :, D + 1:D + 1 + TXT[1]], est[:, s, q * QH:(q + 1) * QH, :],
                                  ALU.mult).then_inc(free_sem(l, f"a{n}"), 1)
                wait_read(dve, l, b, f"a{n}")
                dve.tensor_reduce(n2[:, s, q * QH:(q + 1) * QH], pe_[:, n % 2, :, :], AX_X, ALU.add).then_inc(s_n2, 1)

            def semantic(l, b, n):
                def after(k):
                    b.reached(dve, s_semd, SEMD, k)

                den = ust[:, :, :, D]
                fuv = fu[:].rearrange("p s h n -> p (s h) n")
                fmv = fm[:].rearrange("p s h -> p (s h)")
                fmb = fmv.unsqueeze(2).to_broadcast([P, SC * H, IP])
                nybits, n2bits = ny[:].bitcast(I32), n2[:].bitcast(I32)
                newton = 7
                last = newton + 3 * NEWTON
                if n == 0:
                    b.reached(dve, s_ast, SC * NQ, SC * NQ)
                    dve.tensor_scalar(lim[:], den, EPS / 8, None, ALU.mult).then_inc(s_semd, 1)
                elif n == 1:
                    b.reached(dve, s_n2, SC * NQ, SC * NQ)
                    dve.tensor_scalar(n2[:], n2[:], 1e-37, None, ALU.max).then_inc(s_semd, 1)
                elif n == 2:
                    b.reached(dve, s_at0, 1, 0)
                    dve.reciprocal(rd[1][:], den).then_inc(s_rd[1], 1)
                elif n == 3:
                    after(2)
                    dve.tensor_scalar(nybits, n2bits, 1, None, ALU.logical_shift_right).then_inc(s_semd, 1)
                elif n == 4:
                    after(1)
                    dve.reciprocal(lim[:], lim[:]).then_inc(s_semd, 1)
                elif n == 5:
                    after(3)
                    dve.tensor_scalar(nybits, nybits, -1.0, float(MAGIC), ALU.mult, ALU.add).then_inc(s_semd, 1)
                elif n == 6:
                    rn = rnorm4[:, bass.DynSlice(b.index(), 1), :].to_broadcast([P, SC * H, IP])
                    dve.tensor_tensor(fuv, ast[:].rearrange("p s h n -> p (s h) n"), rn, ALU.mult).then_inc(s_semd, 1)
                elif n < last:
                    after(5 if n == newton else n - 1)
                    if (n - newton) % 3 == 0:
                        dve.tensor_tensor(nt[:], ny[:], ny[:], ALU.mult).then_inc(s_semd, 1)
                    elif (n - newton) % 3 == 1:
                        dve.scalar_tensor_tensor(nt[:], nt[:], -0.5, n2[:], ALU.mult, ALU.mult).then_inc(s_semd, 1)
                    else:
                        dve.scalar_tensor_tensor(ny[:], nt[:], 1.5, ny[:], ALU.add, ALU.mult).then_inc(s_semd, 1)
                elif n == last:
                    after(last - 1)
                    dve.tensor_tensor(ny[:], ny[:], lim[:], ALU.min).then_inc(s_semd, 1)
                elif n == last + 1:
                    after(last)
                    nyb = ny[:].rearrange("p s h -> p (s h)").unsqueeze(2).to_broadcast([P, SC * H, IP])
                    dve.tensor_tensor(fuv, fuv, nyb, ALU.mult).then_inc(s_semd, 1)
                elif n == last + 2:
                    after(last + 1)
                    b.reached(dve, s_sip2, 1, 1)
                    dve.tensor_tensor(fu[:], fu[:], sip2[:], ALU.add).then_inc(s_semd, 1)
                elif n == last + 3:
                    after(last + 2)
                    dve.tensor_reduce(fmv, fuv, AX_X, ALU.max).then_inc(s_semd, 1)
                elif n == last + 4:
                    after(last + 3)
                    dve.tensor_tensor(fuv, fuv, fmb, ALU.subtract).then_inc(s_semd, 1)
                elif n == last + 5:
                    b.reached(dve, s_fe, 1, 1)
                    dve.tensor_reduce(fmv, fuv, AX_X, ALU.add).then_inc(s_semd, 1)
                elif n == last + 6:
                    after(SEMD - 2)
                    dve.reciprocal(fm[:], fm[:]).then_inc(s_semd, 1)
                elif n == last + 7:
                    after(SEMD - 1)
                    dve.tensor_tensor(fm[:], fm[:], mask_sb[:].unsqueeze(2).to_broadcast([P, SC, H]), ALU.mult)\
                       .then_inc(s_semd, 1)
                else:
                    wait_fill(dve, l, b, "pt0", before=True)
                    after(SEMD)
                    dve.tensor_tensor(pip[:].rearrange("p s h n -> p (s h) n"), fuv, fmb, ALU.mult).then_inc(s_pip, 1)

            def attend_ip(l, b, s):
                wait_fill(dve, l, b, f"ip{s}")
                b.reached(dve, s_at0, 1, 1)
                dve.tensor_tensor(at[1][:, s, 0:C], bank(l, f"ip{s}")[:, 0:C], at[1][:, s, 0:C], ALU.add)\
                   .then_inc(free_sem(l, f"ip{s}"), 1)

            def turn_attended(l, b, c):
                m = CC[c][1]
                b.reached(dve, s_ath[l], 3, c + 1)
                low = att[l][:, 1, c, :] if c < 2 else att[l][HALF:P, 0, 2, :]
                dve.tensor_tensor(low, bank(l, f"x{c}")[0:m, 0:S], att[l][0:m, 0, c, :], ALU.subtract)\
                   .then_inc(free_sem(l, f"x{c}"), 1)

            def project(l, b, c):
                m = CC[c][1]
                wait_fill(dve, l, b, f"o{c}")
                o = bank(l, f"o{c}")[0:m, 0:S]
                if l == 0:
                    if c == 0:
                        b.reached(dve, s_res[0], 1, 1)
                        previous(b).reached(dve, s_xl[1], 1, 1)
                        previous(b).reached(dve, s_xt[1], 1, 1)
                        previous(b).reached(dve, s_res[1], 1, 1)
                    dst = xin[1][0:m, c, :]
                else:
                    if c == 0:
                        b.reached(dve, s_moved, 32, 32)
                        b.reached(dve, s_store, 32, 0)
                    dst = outt[0:m, c, :]
                dve.scalar_tensor_tensor(dst, o, 1 / WS, res[l][0:m, c, :], ALU.mult, ALU.add)\
                   .then_inc(free_sem(l, f"o{c}"), 1)

            program(dve, steps_of("dve"), {"xh": high_input, "xt": low_tail, "g": gram, "q": query, "s": scores,
                                           "m": turn_max, "t": turned_scores, "a": attend, "sem": semantic,
                                           "ip": attend_ip, "x": turn_attended, "o": project}, {0: lambda: clear(1)})

        @block.gpsimd
        def _(pool):
            def clear(l):
                for t in pool_clears[l]:
                    pool.memset(t[:], 0.0).then_inc(s_zero_pool, 1)

            clear(0)
            pool.memset(one[:], 1.0).then_inc(s_zero_pool, 1)
            pool.wait_ge(s_w, 16 * WEIGHTS)
            pool.wait_ge(s_zero_pool, POOL_FIRST)

            def high_input(l, b, n):
                b.reached(pool, s_x, 32, 32)
                wait_fill(pool, l, b, "q2", before=True)
                pool.tensor_tensor(xs[l][:, 0, :, :], xin[l][:], one[:, 0:1].unsqueeze(2).to_broadcast([P, 3, S]),
                                   ALU.mult).then_inc(s_xh[l], 1)

            def low_input(l, b, n):
                b.reached(pool, s_xh[l], 1, 1)
                pool.tensor_tensor(xs[l][:, 1, 0:2, :], xin[l][:, 0:2, :], xs[l][:, 0, 0:2, :], ALU.subtract)\
                    .then_inc(s_xl[l], 1)

            def values(l, b, n):
                b.reached(pool, s_vst[l], 16, 16)
                if l == 0 and b.fixed:
                    pool.wait_ge(s_zero_dve, DVE_FIRST)
                wait_fill(pool, l, b, f"a{AV[l] - 1}", before=True)
                m = TXT[l]
                for h, t in enumerate((vh[l], vl[l])):
                    pool.tensor_tensor(t[0:m, :, 0:D], vst[l][0:m, h, :].rearrange("t (h d) -> t h d", d=D),
                                       one[0:m, :].unsqueeze(2).to_broadcast([m, H, D]), ALU.mult).then_inc(s_v[l], 1)

            def residual(l, b, c):
                m = CC[c][1]
                if l == 0:
                    if c == 0:
                        b.reached(pool, s_x, 32, 32)
                    wait_read(pool, 0, b, f"o{c}", before=True)
                    dst = res[0]
                else:
                    wait_read(pool, 0, b, f"o{c}")
                    if c == 0:
                        b.reached(pool, s_moved, 32, 0)
                    dst = res_next
                ins = pool.tensor_tensor(dst[0:m, c, :], xin[l][0:m, c, :],
                                         bias_sb[l][0:m, c:c + 1].to_broadcast([m, S]), ALU.add)
                if c == len(CC) - 1:
                    ins.then_inc(s_res[l], 1)

            def ip_values(l, b, n):
                b.reached(pool, s_viprow, 16, 16)
                wait_fill(pool, l, b, "ip1", before=True)
                pool.tensor_tensor(vbip[0:H * IP, :].rearrange("k (h d) -> k h d", d=D),
                                   viprow[:].rearrange("k (h d) -> k h d", d=D),
                                   ipmask[:].unsqueeze(2).to_broadcast([H * IP, H, D]), ALU.mult).then_inc(s_vb, 1)

            def turned_scores(l, b, p):
                low_parts(pool, l, b, p)

            def keep_ip_scores(l, b, n):
                b.reached(pool, s_sip, SC * G, SC * G)
                b.reached(pool, s_semd, SEMD, 0)
                pool.tensor_tensor(sip2[:], sip[:], one[:].unsqueeze(1).unsqueeze(3).to_broadcast([P, SC, H, IP]),
                                   ALU.mult).then_inc(s_sip2, 1)

            def attended_text(l, b, n):
                wait_fill(pool, l, b, "x2", before=True)
                b.reached(pool, s_rd[1], 1, 1)
                pool.tensor_tensor(at[1][:, :, 0:C].rearrange("p s (h d) -> p s h d", d=D), ust[:, :, :, 0:D],
                                   rd[1][:].unsqueeze(3).to_broadcast([P, SC, H, D]), ALU.mult).then_inc(s_at0, 1)

            program(pool, steps_of("pool"), {"ks": keep_ip_scores, "at": attended_text, "xh": high_input,
                                             "xl": low_input, "v": values, "res": residual, "vb": ip_values,
                                             "t": turned_scores}, {0: lambda: clear(1)})


def attention_stack_kernel(nc, x, ctx, ctxip, mask, wq, wk, wv, wo, bias, wk_ip, wv_ip, ident_d, ident16_d, ipmask_d,
                           ind_d, out):
    both = (0, 1)
    k_dram = [nc.dram_tensor(f"k_dram{l}", (2, C, B * T), F16, kind="Internal").ap() for l in both]
    v_dram = [nc.dram_tensor(f"v_dram{l}", (B * T, 2 * C), F16, kind="Internal").ap() for l in both]
    g_dram = nc.dram_tensor("g_dram", (B, TXT[1], 2 * T), F16, kind="Internal").ap()
    vip_dram = nc.dram_tensor("vip_dram", (B * IP, C), F32, kind="Internal").ap()
    with ExitStack() as stack:
        def sb(name, shape, dt=F32):
            return stack.enter_context(nc.sbuf_tensor(name, shape, dt))
        psum = stack.enter_context(nc.psum_tensor("psum", [P, RING, 512], F32))
        wqs = [sb(f"wq{l}", [P, 2, 3, C], F16) for l in both]
        wos = [sb(f"wo{l}", [P, 2, 3, C], F16) for l in both]
        rnorm4 = sb("rnorm4", [P, B, IP])
        keys_and_values(nc, psum, ctx, ctxip, wk, wv, wq, wo, wk_ip, wv_ip, k_dram, v_dram, g_dram, vip_dram, wqs, wos,
                        rnorm4)
        attention(nc, psum, x, mask, bias, ident_d, ident16_d, ipmask_d, ind_d, k_dram, v_dram, g_dram, vip_dram, wqs,
                  wos, rnorm4, out)


_OUT = (B, C, S)


def kernel(x, ctx_2048, fside_S_0, L0_xattn_Wq, L0_xattn_Wk, L0_xattn_Wv, L0_xattn_Wk_ip, L0_xattn_Wv_ip, L0_xattn_Wo,
           L0_xattn_bo, L1_xattn_W_q, L1_xattn_W_k, L1_xattn_W_v, L1_xattn_W_k_ip, L1_xattn_W_v_ip, L1_xattn_W_out,
           L1_xattn_b_out):
    from concourse import bacc
    from concourse.bass_utils import run_bass_kernel_spmd

    def turned(a):
        return np.ascontiguousarray(np.swapaxes(np.asarray(a), -1, -2))

    ctxt = np.moveaxis(np.asarray(ctx_2048), 2, 0)
    heads = np.arange(H)
    ind = np.zeros((HALF, GH, G, T), np.float16)
    ind[heads, heads % GH, heads // GH] = 1
    arrays = {
        "x": turned(x), "ctx": np.ascontiguousarray(ctxt).reshape(E, B * T),
        "ctxip": np.ascontiguousarray(ctxt[:, :, TXT[1]:]).reshape(E, B * IP),
        "mask": np.ascontiguousarray(np.asarray(fside_S_0).reshape(SC, P).T),
        "wq0": turned(L0_xattn_Wq), "wq1": np.asarray(L1_xattn_W_q),
        "wk0": turned(L0_xattn_Wk), "wk1": np.asarray(L1_xattn_W_k),
        "wv0": turned(L0_xattn_Wv), "wv1": np.asarray(L1_xattn_W_v),
        "wo0": turned(L0_xattn_Wo), "wo1": np.asarray(L1_xattn_W_out),
        "bias0": np.asarray(L0_xattn_bo).reshape(C, 1), "bias1": np.asarray(L1_xattn_b_out).reshape(C, 1),
        "wk_ip": np.asarray(L1_xattn_W_k_ip), "wv_ip": np.asarray(L1_xattn_W_v_ip),
        "ident": np.eye(P, dtype=np.float32), "ident16": np.eye(P, dtype=np.float16),
        "ipmask": (np.arange(H * IP)[:, None] // IP == heads).astype(np.float32),
        "ind": ind.reshape(HALF, H * T),
    }
    nc = bacc.Bacc("TRN2", target_bir_lowering=False, num_devices=1)
    ap = {n: nc.dram_tensor(f"in_{n}", a.shape, mybir.dt.from_np(a.dtype), kind="ExternalInput").ap()
          for n, a in arrays.items()}
    out = nc.dram_tensor("out", _OUT, F32, kind="ExternalOutput").ap()
    attention_stack_kernel(
        nc, ap["x"], ap["ctx"], ap["ctxip"], ap["mask"], (ap["wq0"], ap["wq1"]), (ap["wk0"], ap["wk1"]),
        (ap["wv0"], ap["wv1"]), (ap["wo0"], ap["wo1"]), (ap["bias0"], ap["bias1"]), ap["wk_ip"], ap["wv_ip"],
        ap["ident"], ap["ident16"], ap["ipmask"], ap["ind"], out)
    r = run_bass_kernel_spmd(nc, [{f"in_{n}": a for n, a in arrays.items()}], core_ids=[0])
    return turned(r.results[0]["out"])
```
